# Optimizing a Trainium2 kernel written in Bass

```python
import numpy as np
import jax
import jax.numpy as jnp

def _softmax(x, axis=-1):
    return jax.nn.softmax(x, axis=axis)

def _gelu(x):
    return jax.nn.gelu(x, approximate=True)

def _silu(x):
    return jax.nn.silu(x)

def _sigmoid(x):
    return jax.nn.sigmoid(x)

def _layernorm(x, axis=-1, eps=1e-05):
    m = jnp.mean(x, axis=axis, keepdims=True)
    v = jnp.var(x, axis=axis, keepdims=True)
    return (x - m) / jnp.sqrt(v + eps)

def _scatter_add(tgt, idx, src, axis=0):
    return tgt.at[idx].add(src)

def _segment_sum(src, seg, n):
    return jax.ops.segment_sum(src, seg, n)
kernel_name = 'mk_gnn_preln_d2_gnn_r8_437359'

def setup_inputs(seed: int=0):
    np.random.seed(seed)
    _w = jnp.asarray

    def _rec_inputs():
        import jax
        import jax.numpy as jnp
        _gk = jax.random.key(seed)
        x = -0.0003713 + 1 * jax.random.normal(jax.random.fold_in(_gk, 1), (12500, 128), jnp.float32)
        src = jax.random.randint(jax.random.fold_in(_gk, 2), (400000,), 0, 12500, jnp.int32)
        dst = jnp.minimum((12500 * jax.random.uniform(jax.random.fold_in(_gk, 3), (400000,)) ** 2.0).astype(jnp.int32), 99999)
        _o = jnp.argsort(dst, stable=True)
        src = src[_o]
        dst = dst[_o]
        edge_attr_4 = -0.000107899 + 1.00008 * jax.random.normal(jax.random.fold_in(_gk, 11), (400000, 4), jnp.float32)
        edge_attr_8 = jax.random.uniform(jax.random.fold_in(_gk, 12), (400000, 8), jnp.float32, 0.0, 1)
        edge_weight = jax.random.uniform(jax.random.fold_in(_gk, 14), (400000,), jnp.float32, 0.0, 0.999998)
        return (x, src, dst, edge_attr_4, edge_attr_8, edge_weight)
    x, src, dst, edge_attr_4, edge_attr_8, edge_weight = _rec_inputs()

    def _L0_gnn_setup():
        import jax, jax.numpy as jnp
        import numpy as np
        N_NODES = 12500
        N_EDGES = 80000
        DIM = 128
        key = jax.random.key(seed)
        k1, k2, k3, k4, k5 = jax.random.split(key, 5)
        x = jax.random.normal(k1, (N_NODES, DIM), dtype=jnp.float32)
        edge_index = jax.random.randint(k2, (2, N_EDGES), 0, N_NODES, dtype=jnp.int64)
        edge_weight = jax.random.uniform(k3, (N_EDGES,), dtype=jnp.float32)
        W = jax.random.normal(k4, (DIM, DIM), dtype=jnp.float32) * (1.0 / np.sqrt(DIM))
        b = jax.random.normal(k5, (DIM,), dtype=jnp.float32) * 0.01
        return {'x': x, 'edge_index': edge_index, 'edge_weight': edge_weight, 'W': W, 'b': b}
    _L0_gnn_all = _L0_gnn_setup()
    _L0_gnn_in = {k: v for k, v in _L0_gnn_all.items() if k in ('W', 'b')}
    del _L0_gnn_all

    def _L1_gnn_setup():
        import jax, jax.numpy as jnp
        import numpy as np
        MUL = 32
        N_NODES = 6250
        N_EDGES = 100000
        R3 = np.sqrt(3.0).astype(np.float32)
        key = jax.random.key(seed)
        ks = jax.random.split(key, 12)
        inp = {}
        inp['node_feats'] = jax.random.normal(ks[0], (N_NODES, 4 * MUL), dtype=jnp.float32)
        inp['edge_attrs'] = jax.random.normal(ks[1], (N_EDGES, 4), dtype=jnp.float32)
        inp['edge_feats'] = jax.random.uniform(ks[2], (N_EDGES, 8), dtype=jnp.float32)
        inp['edge_index'] = jax.random.randint(ks[3], (2, N_EDGES), 0, N_NODES)
        inp['W_up_s'] = jax.random.normal(ks[4], (MUL, MUL), dtype=jnp.float32)
        inp['W_up_v'] = jax.random.normal(ks[5], (MUL, MUL), dtype=jnp.float32)
        inp['A1'] = jax.random.normal(ks[6], (8, 64), dtype=jnp.float32) / np.sqrt(8.0)
        inp['b1'] = jnp.zeros((64,), dtype=jnp.float32)
        inp['A2'] = jax.random.normal(ks[7], (64, 64), dtype=jnp.float32) / np.sqrt(64.0)
        inp['b2'] = jnp.zeros((64,), dtype=jnp.float32)
        inp['A3'] = jax.random.normal(ks[8], (64, 4 * MUL), dtype=jnp.float32) * (10.0 * np.sqrt(6.0 / (64 + 4 * MUL)))
        inp['W_out_s'] = jax.random.normal(ks[9], (2 * MUL, MUL), dtype=jnp.float32)
        inp['W_out_v'] = jax.random.normal(ks[10], (2 * MUL, MUL), dtype=jnp.float32)
        return inp
    _L1_gnn_all = _L1_gnn_setup()
    _L1_gnn_in = {k: v for k, v in _L1_gnn_all.items() if k in ('W_up_s', 'W_up_v', 'A1', 'b1', 'A2', 'b2', 'A3', 'W_out_s', 'W_out_v')}
    del _L1_gnn_all
    return {'x': x, 'src': src, 'dst': dst, 'edge_attr_4': edge_attr_4, 'edge_attr_8': edge_attr_8, 'edge_weight': edge_weight, 'L0_gnn_W': _L0_gnn_in['W'], 'L0_gnn_b': _L0_gnn_in['b'], 'L1_gnn_W_up_s': _L1_gnn_in['W_up_s'], 'L1_gnn_W_up_v': _L1_gnn_in['W_up_v'], 'L1_gnn_A1': _L1_gnn_in['A1'], 'L1_gnn_b1': _L1_gnn_in['b1'], 'L1_gnn_A2': _L1_gnn_in['A2'], 'L1_gnn_b2': _L1_gnn_in['b2'], 'L1_gnn_A3': _L1_gnn_in['A3'], 'L1_gnn_W_out_s': _L1_gnn_in['W_out_s'], 'L1_gnn_W_out_v': _L1_gnn_in['W_out_v']}

def reference(x, src, dst, edge_attr_4, edge_attr_8, edge_weight, L0_gnn_W, L0_gnn_b, L1_gnn_W_up_s, L1_gnn_W_up_v, L1_gnn_A1, L1_gnn_b1, L1_gnn_A2, L1_gnn_b2, L1_gnn_A3, L1_gnn_W_out_s, L1_gnn_W_out_v):
    import jax
    import jax.numpy as jnp

    def _L0_gnn_ref(x, edge_index, edge_weight, W, b):
        import jax, jax.numpy as jnp
        import numpy as np
        N_NODES = 12500
        N_EDGES = 80000
        DIM = 128
        row, col = (edge_index[0], edge_index[1])
        msgs = edge_weight[:, None] * x[row]
        agg = jax.ops.segment_sum(msgs, col, num_segments=x.shape[0])
        return agg @ W.T + b

    def _L1_gnn_ref(node_feats, edge_attrs, edge_feats, W_up_s, W_up_v, A1, b1, A2, b2, A3, W_out_s, W_out_v, edge_index):
        import jax, jax.numpy as jnp
        import numpy as np
        MUL = 32
        N_NODES = 6250
        N_EDGES = 100000
        R3 = np.sqrt(3.0).astype(np.float32)
        num_nodes = node_feats.shape[0]
        sender, receiver = (edge_index[0], edge_index[1])
        s = node_feats[:, :MUL]
        v = node_feats[:, MUL:].reshape(num_nodes, MUL, 3)
        inv = 1.0 / np.sqrt(MUL).astype(np.float32)
        s = s @ W_up_s * inv
        v = jnp.einsum('nui,uw->nwi', v, W_up_v) * inv
        h = jax.nn.silu(edge_feats @ A1 + b1)
        h = jax.nn.silu(h @ A2 + b2)
        tpw = h @ A3
        w0, w1, w2, w3 = jnp.split(tpw, 4, axis=1)
        ss = s[sender]
        vs = v[sender]
        y_s = edge_attrs[:, :1]
        y_v = edge_attrs[:, 1:4]
        out_s0 = ss * y_s * w0
        out_s3 = jnp.einsum('eui,ei->eu', vs, y_v) / R3 * w3
        out_v1 = ss[:, :, None] * y_v[:, None, :] * w1[:, :, None]
        out_v2 = vs * y_s[:, :, None] * w2[:, :, None]
        E = ss.shape[0]
        mji = jnp.concatenate([out_s0, out_s3, out_v1.reshape(E, 3 * MUL), out_v2.reshape(E, 3 * MUL)], axis=1)
        message = jax.ops.segment_sum(mji, receiver, num_segments=num_nodes) / 10.0
        ms = message[:, :2 * MUL]
        mv = message[:, 2 * MUL:].reshape(num_nodes, 2 * MUL, 3)
        inv2 = 1.0 / np.sqrt(2 * MUL).astype(np.float32)
        out_s = ms @ W_out_s * inv2
        out_v = jnp.einsum('nui,uw->nwi', mv, W_out_v) * inv2
        return jnp.concatenate([out_s, out_v.reshape(num_nodes, 3 * MUL)], axis=1)
    edge_index = jnp.stack([src, dst])
    h = jnp.maximum(_layernorm(x, axis=-1), 0.0)
    x = x + _L0_gnn_ref(h, edge_index, edge_weight, L0_gnn_W, L0_gnn_b)
    h = jnp.maximum(_layernorm(x, axis=-1), 0.0)
    x = x + _L1_gnn_ref(h, edge_attr_4, edge_attr_8, L1_gnn_W_up_s, L1_gnn_W_up_v, L1_gnn_A1, L1_gnn_b1, L1_gnn_A2, L1_gnn_b2, L1_gnn_A3, L1_gnn_W_out_s, L1_gnn_W_out_v, edge_index)
    return x

_drawn_inputs = setup_inputs


def setup_inputs(seed=0):
    import zlib

    import numpy as np

    out = dict(_drawn_inputs(seed))
    spreads = {'L1_gnn_b1': (0.0, 0.512), 'L1_gnn_b2': (0.0, 0.1)}
    factors = {'L0_gnn_b': 60.741}
    for name, (base, spread) in spreads.items():
        noise = np.random.default_rng([zlib.crc32(name.encode()), seed]).standard_normal(out[name].shape)
        drawn = base * np.exp(spread * noise) if base else spread * noise
        out[name] = jnp.asarray(drawn.astype(out[name].dtype))
    for name, factor in factors.items():
        out[name] = (out[name] * factor).astype(out[name].dtype)
    return out
```

```python
import math

import concourse.bass as bass
from concourse import mybir
from contextlib import ExitStack

P = 128
SLOTS = 16
ITEMS = SLOTS // 2
QUADS = SLOTS // 4
CHUNKS = 8
MACRO_ITEMS = CHUNKS * ITEMS
assert MACRO_ITEMS * 2 == P
MUL = 32
NE8 = 8


def divisor(n, most):
    return max(d for d in range(1, most + 1) if n % d == 0)


def build_gnn(nc, x, src, dst, ea4, ea8, ew, W, b, Wus, Wuv, A1, b1, A2, b2, A3, Wos, Wov, out):
    f32, i32 = mybir.dt.float32, mybir.dt.int32
    ALU, ACT, AX = mybir.AluOpType, mybir.ActivationFunctionType, mybir.AxisListType
    ds = bass.ds

    N, E = x.shape[0], src.shape[0]
    NB = -(-N // P)
    TAIL = N - (NB - 1) * P
    TILES = E // P
    assert E % P == 0 and x.shape[1] == P
    PAIRS = -(-TILES // 2)
    FULL = E // (2 * P)
    MACROS = -(-(PAIRS + NB - 1) // MACRO_ITEMS)
    COLS = MACROS + 2
    NCH = MACROS * CHUNKS
    NIT = MACROS * MACRO_ITEMS
    GB = divisor(NB, min(8, NB // 4))
    NBG = NB // GB
    GW = GB * P
    EPS = 1e-5
    INV_UP = 1.0 / math.sqrt(MUL)
    INV_OUT = 1.0 / math.sqrt(2 * MUL) / 10.0
    INV_R3 = 1.0 / math.sqrt(3.0)
    NOWHERE = 1.0e6
    R1 = divisor(E, P)
    C1 = E // R1
    R2 = divisor(FULL, P)
    C2 = FULL // R2
    ROW = NIT + 8
    FREE = ITEMS

    src_rows = src.rearrange("(t e) -> t e", e=P)
    dst_rows = dst.rearrange("(t e) -> t e", e=P)
    ew_rows = ew.rearrange("(t e) -> t e", e=P)
    ea4_rows = ea4.rearrange("(t e) c -> t (e c)", e=P)
    ea8_rows = ea8.rearrange("(t e) c -> t (e c)", e=P)

    h0_table = nc.dram_tensor("h0_table", (NB * P, P), f32, kind="Internal").ap()
    up_table = nc.dram_tensor("up_table", (NB * P, P), f32, kind="Internal").ap()
    x1_table = nc.dram_tensor("x1_table", (NB * P, P), f32, kind="Internal").ap()
    blocks_dram = nc.dram_tensor("blocks_dram", (COLS, MACRO_ITEMS), f32, kind="Internal").ap()

    with ExitStack() as ctx:
        def sb(name, shape, dt=f32):
            return ctx.enter_context(nc.sbuf_tensor(name, shape, dt))

        def sem(name):
            return ctx.enter_context(nc.semaphore(name))

        zeros = sb("zeros", [P, P])
        arena = sb("arena", [P, max(NB * P, 12160 + 2 * GB * P)])
        agg = sb("agg", [P, NB * 2 * P])
        ident = sb("ident", [P, P])
        ones = sb("ones", [P, P])
        iota_free = sb("iota_free", [P, P])
        w_t = sb("w_t", [P, P])
        bias_row = sb("bias_row", [1, P])
        w_up = sb("w_up", [P, P])
        a1_blocks = sb("a1_blocks", [P, NE8, P])
        a2_pair = sb("a2_pair", [P, P])
        a3_pair = sb("a3_pair", [P, 2 * P])
        b1_col = sb("b1_col", [P, 1])
        b2_col = sb("b2_col", [P, 1])
        w_out = sb("w_out", [P, 2, P])
        item_of = sb("item_of", [P, COLS])
        block_of = sb("block_of", [P, COLS])
        tile_f = sb("tile_f", [P, COLS])
        late = sb("late", [P, COLS])
        tile_i = sb("tile_i", [P, COLS], i32)
        tile_odd_i = sb("tile_odd_i", [P, COLS], i32)
        shift = sb("shift", [P, COLS])
        small = sb("small", [P, 24])
        small_i = sb("small_i", [P, 4], i32)
        flag = sb("flag", [P, 4])
        row_f = sb("row_f", [1, ROW])
        row_i = sb("row_i", [1, ROW], i32)
        stats = sb("stats", [P, GB, 6])
        moments = sb("moments", [P, GB, 2])
        spread = sb("spread", [P, 2, GB])
        scales = sb("scales", [P, 2, GB])
        meta_col = sb("meta_col", [P, 2], i32)
        raw_src = sb("raw_src", [P, P], i32)
        raw_dst = sb("raw_dst", [P, P], i32)
        raw_w = sb("raw_w", [P, P])
        src_f = sb("src_f", [P, P])
        dst_f = sb("dst_f", [P, P])
        src_t = sb("src_t", [P, 2, P])
        dst_t = sb("dst_t", [P, 2, P])
        w_edge = sb("w_edge", [P, 2, P])
        picks = sb("picks", [P, SLOTS], i32)
        rows = sb("rows", [P, SLOTS, P])
        hot = sb("hot", [P, 2, 2, P])

        place = [0]

        def part(width):
            place[0] += width
            assert place[0] <= arena.shape[1]
            return arena[:, place[0] - width:place[0]]

        raw_ea = part(4 * P)
        raw_ef = part(2 * NE8 * P).rearrange("p (k w) -> p k w", k=2)[0:64]
        ef_pair = part(2 * NE8 * P).rearrange("p (b k w) -> p b k w", b=16, k=2)[0:64]
        ef_t = part(16 * P).rearrange("p (b q) -> p b q", b=16)
        y_edge = part(4 * 2 * P).rearrange("p (c k q) -> p c k q", c=4, k=2)
        hid1 = part(ITEMS * P).rearrange("p (q e) -> p q e", q=ITEMS)
        hid2 = part(ITEMS * P).rearrange("p (q e) -> p q e", q=ITEMS)
        SP = 22
        scaled = part(2 * SP * MUL).rearrange("p (a c u) -> p a c u", a=2, c=SP)
        msg = part(2 * 4 * P).rearrange("p (a r c u) -> p a r c u", a=2, r=4, c=4)

        fin_x1 = part(GW)
        fin_st = part(GW)
        fin_sums = rows[:, :, :].rearrange("p s d -> p (s d)")[:, 0:2 * GW]
        spare = lambda i: agg[:, NB * P + i * GW:NB * P + (i + 1) * GW]
        sums_st, h_st, h_turn, up_st = (spare(i) for i in range(4))
        started = agg[:, NB * P:NB * P + COLS * (NB - 1)].rearrange("p (c b) -> p c b", c=COLS)
        HALVES = [(0, min(GW, 512)), (min(GW, 512), GW)]
        HALVES = [h for h in HALVES if h[1] > h[0]]
        where = lambda g: (g * P // 512, g * P % 512)

        bank = [ctx.enter_context(nc.psum_tensor(f"bank{i}", [P, 512], f32)) for i in range(8)]
        b_w = [bank[0], bank[2]]
        b_sum = [bank[4], bank[5]]
        b_mlp, b_turn = bank[6], bank[7]

        x_zeroed = sem("x_zeroed")
        x_in = sem("x_in")
        order_in = sem("order_in")
        w_zeroed = sem("w_zeroed")
        w_in = sem("w_in")
        consts = sem("consts")
        votes = sem("votes")
        counted = sem("counted")
        chain = sem("chain")
        passes_ready = sem("passes_ready")
        plan_out = sem("plan_out"); plan_stored = sem("plan_stored"); plan_in = sem("plan_in")
        pool_turn = sem("pool_turn"); act_turn = sem("act_turn"); dve_turn = sem("dve_turn")
        pe_turn = sem("pe_turn")
        stats_done = sem("stats_done"); var_ready = sem("var_ready"); sd_ready = sem("sd_ready")
        ln_ready = sem("ln_ready")
        normed = sem("normed")
        h_stored = sem("h_stored"); h_saved = sem("h_saved")
        table_ready = sem("table_ready")
        sums_in = sem("sums_in")
        lin_ready = sem("lin_ready"); x1_ready = sem("x1_ready"); x1_stored = sem("x1_stored")
        h_turned = sem("h_turned"); h_copied = sem("h_copied")
        up_ready = sem("up_ready"); up_out = sem("up_out"); up_stored = sem("up_stored"); up_saved = sem("up_saved")
        fin_staged = sem("fin_staged"); fin_x = sem("fin_x"); fin_ready = sem("fin_ready")
        fin_out = sem("fin_out"); fin_stored = sem("fin_stored"); fin_saved = sem("fin_saved")

        class Layer:
            def __init__(self, n):
                s = lambda name: sem(f"{name}_{n}")
                self.n = n
                self.rounds = (1, 4)[n]
                self.fetches = (3, 5)[n]
                self.table = (h0_table, up_table)[n]
                self.plan = s("plan")
                self.plan_step = s("plan_step")
                self.col_ready = s("col_ready")
                self.meta_in = s("meta_in")
                self.floats = s("floats")
                self.turned = s("turned")
                self.turned_out = s("turned_out")
                self.picks_ready = s("picks_ready")
                self.quad = [s(f"quad{q}") for q in range(QUADS)]
                self.hot_ready = s("hot_ready")
                self.sums = s("sums")
                self.added = s("added")
                self.walked = s("walked")
                if n == 1:
                    self.paired = s("paired")
                    self.mlp = s("mlp")
                    self.mlp_out = s("mlp_out")
                    self.weights = s("weights")
                    self.scaled = s("scaled")
                    self.dots = s("dots")
                    self.mixed = s("mixed")
                self.used = self.sums if n == 0 else self.scaled

            def used_before(self, p):
                return p * (NIT + 1) + 1 + FREE if self.n == 0 else p * NIT + FREE

            def sums_before(self, p):
                return p * (NIT + 1) + (FREE if self.n == 0 else 0)

            def preps_before(self, p):
                return p * (MACROS + 1)

        layers = [Layer(0), Layer(1)]

        def after(eng, turn, semaphore, value):
            eng.wait_ge(semaphore, value)
            eng.sem_inc(turn, 1)

        loads = [(bias_row[:, :], b.rearrange("(a n) -> a n", a=1)), (w_up[0:MUL, 0:MUL], Wus)]
        for i in range(3):
            loads.append((w_up[MUL + i:MUL + i + 3 * MUL - 2:3, MUL * (i + 1):MUL * (i + 2)], Wuv))
        for k in range(2):
            lo = 64 * k
            for e in range(NE8):
                loads.append((a1_blocks[lo + 8 * e:lo + 8 * e + 8, e, lo:lo + 64], A1))
            loads.append((a2_pair[lo:lo + 64, lo:lo + 64], A2))
            for at, w in ((2 * k, 2), (2 * k + 1, 1), (2 * k + 4, 0), (2 * k + 5, 3)):
                loads.append((a3_pair[lo:lo + 64, MUL * at:MUL * (at + 1)], A3[:, MUL * w:MUL * (w + 1)]))
            loads.append((b1_col[lo:lo + 64, :], b1.rearrange("(n a) -> n a", a=1)))
            loads.append((b2_col[lo:lo + 64, :], b2.rearrange("(n a) -> n a", a=1)))
            loads.append((raw_w[0:MUL, MUL * k:MUL * (k + 1)], Wos[MUL * k:MUL * (k + 1), :]))
            for i in range(3):
                loads.append((raw_w[MUL * (i + 1):MUL * (i + 2), MUL * k:MUL * (k + 1)],
                              Wov[MUL * (1 - k):MUL * (2 - k), :]))

        block = ctx.enter_context(nc.Block())

        @block.sync
        def _(sp):
            rows_of = lambda table, t: table[ds(t * GW, GW), :].rearrange("(b p) d -> p b d", p=P)
            cut = lambda ap: ap.rearrange("p (b d) -> p b d", d=P)
            sp.dma_start(agg[0:R1, 0:C1].bitcast(i32), dst.rearrange("(r c) -> r c", r=R1)).then_inc(order_in, 16)
            sp.dma_start(agg[0:R2, C1:C1 + 2 * P * C2].bitcast(i32),
                         dst[0:FULL * 2 * P].rearrange("(r c) -> r c", r=R2)).then_inc(order_in, 16)
            sp.dma_start(small_i[0:R1 - 1, 0:1], dst.rearrange("(r c) -> r c", r=R1)[1:R1, 0:1],
                         allow_slow_non_contiguous=True).then_inc(order_in, 16)
            sp.dma_start(w_t[:, :], W).then_inc(order_in, 16)
            sp.wait_ge(x_zeroed, 1)
            sp.dma_start(cut(arena[:, 0:(NB - 1) * P]),
                         x[0:(NB - 1) * P, :].rearrange("(b p) d -> p b d", p=P)).then_inc(x_in, 16)
            sp.dma_start(arena[0:TAIL, (NB - 1) * P:NB * P], x[(NB - 1) * P:N, :]).then_inc(x_in, 16)
            sp.wait_ge(w_zeroed, 1)
            for to, of in loads:
                sp.dma_start(to, of).then_inc(w_in, 16)
            sp.wait_ge(plan_out, 1)
            sp.dma_start(blocks_dram, agg[0:COLS, 0:MACRO_ITEMS]).then_inc(plan_stored, 16)
            sp.wait_ge(plan_stored, 16)
            sp.dma_start(row_f[0:1, 1:NIT + 1],
                         blocks_dram[0:MACROS, :].rearrange("(a m) q -> a (m q)", a=1)).then_inc(plan_in, 16)
            sp.sem_inc(h_saved, 2)
            with sp.Fori(0, NBG) as t:
                sp.wait_ge(normed, t + 2)
                sp.dma_start(rows_of(h0_table, t), cut(agg[:, ds(NB * P + (t % 2) * GW, GW)])).then_inc(h_stored, 16)
                after(sp, h_saved, h_stored, 16 * t + 16)
            sp.sem_inc(table_ready, 1)
            sp.sem_inc(up_saved, 1)
            with sp.Fori(0, NBG) as t:
                sp.wait_ge(x1_ready, t + 2)
                sp.dma_start(rows_of(x1_table, t), cut(arena[:, ds(t * GW, GW)])).then_inc(x1_stored, 16)
                sp.wait_ge(up_out, t + 2)
                sp.dma_start(rows_of(up_table, t), cut(up_st)).then_inc(up_stored, 16)
                sp.wait_ge(x1_stored, 16 * t + 16)
                after(sp, up_saved, up_stored, 16 * t + 16)
            sp.sem_inc(table_ready, 1)
            sp.sem_inc(fin_saved, 1)
            sp.wait_ge(layers[1].walked, 1)

            def load_x1(t):
                sp.wait_ge(fin_out, t + 1)
                sp.dma_start(cut(fin_x1), rows_of(x1_table, t)).then_inc(fin_x, 16)

            with sp.Fori(0, NBG - 1) as t:
                load_x1(t)
                sp.wait_ge(fin_out, t + 2)
                sp.dma_start(rows_of(out, t), cut(fin_st)).then_inc(fin_stored, 16)
                after(sp, fin_saved, fin_stored, 16 * t + 16)
            load_x1(NBG - 1)
            sp.wait_ge(fin_out, NBG + 1)
            last = (NBG - 1) * GW
            if GB > 1:
                sp.dma_start(out[last:last + GW - P, :].rearrange("(b p) d -> p b d", p=P),
                             cut(fin_st[:, 0:GW - P])).then_inc(fin_stored, 16)
            sp.dma_start(out[last + GW - P:N, :], fin_st[0:TAIL, GW - P:GW]).then_inc(fin_stored, 16)
            sp.wait_ge(fin_stored, 16 * (NBG - 1 + (2 if GB > 1 else 1)))

        @block.gpsimd
        def _(pool):
            nc.gpsimd.memset(ones[:, :], 1.0).then_inc(consts, 1)
            exact = dict(allow_small_or_imprecise_dtypes=True)
            nc.gpsimd.iota(iota_free[:, :], [[1, P]], base=0, channel_multiplier=0, **exact).then_inc(consts, 1)
            nc.gpsimd.iota(item_of[:, :], [[MACRO_ITEMS, COLS]], base=0, channel_multiplier=0, **exact).then_inc(consts, 1)
            nc.gpsimd.iota(small_i[:, 1:2], [[1, 1]], base=0, channel_multiplier=1).then_inc(consts, 1)
            nc.gpsimd.iota(hot[:, 0, 0, 0:NB - 1], [[P, NB - 1]], base=P, channel_multiplier=0, **exact).then_inc(consts, 1)
            pool.wait_ge(consts, 5)
            nc.gpsimd.affine_select(out=ident[:, :], in_=ones[:, :], compare_op=ALU.is_equal, fill=0.0,
                                    base=0, pattern=[[-1, P]], channel_multiplier=1).then_inc(consts, 1)
            pool.wait_ge(passes_ready, 1)
            passes = pool.value_load(small_i[0:1, 2:3], min_val=1, max_val=NB)

            def fetch(L, p, macro):
                after(pool, pool_turn, L.turned, L.rounds * (L.preps_before(p) + macro) + 1)
                nc.gpsimd.tensor_copy(meta_col[:, 0:1], tile_i[:, ds(macro, 1)]).then_inc(L.col_ready, 1)
                nc.gpsimd.tensor_copy(meta_col[:, 1:2], tile_odd_i[:, ds(macro, 1)]).then_inc(L.col_ready, 1)
                after(pool, pool_turn, L.col_ready, 2 * (p * (MACROS + 2) + macro) + 2)
                every = [(raw_src[:, :], src_rows, P, 0), (raw_dst[:, :], dst_rows, P, 0)]
                if L.n == 0:
                    every += [(raw_w[:, :], ew_rows, P, 0)]
                else:
                    every += [(raw_ea, ea4_rows, P, 0), (raw_ef[:, 0, :], ea8_rows, 64, 0),
                              (raw_ef[:, 1, :], ea8_rows, 64, 1)]
                for to, of, parts, col in every:
                    pool.indirect_dma_start(
                        out=to, out_offset=None, in_=of,
                        in_offset=bass.IndirectOffsetOnAxis(ap=meta_col[0:parts, col:col + 1], axis=0),
                    ).then_inc(L.meta_in, 16)

            for L in layers:
                pool.sem_inc(L.turned, 1)
                pool.sem_inc(L.used, FREE)
                pool.wait_ge(table_ready, L.n + 1)
                with pool.Fori(0, passes) as p:
                    after(pool, pool_turn, L.plan, p + 1)
                    fetch(L, p, 0)
                    fetch(L, p, 1)
                    with pool.Fori(0, MACROS) as m:
                        with pool.Fori(0, CHUNKS) as c:
                            chunk = m * CHUNKS + c
                            for q in range(QUADS):
                                after(pool, pool_turn, L.picks_ready, QUADS * (p * (NCH + 1) + chunk) + q + 1)
                                after(pool, pool_turn, L.used,
                                      L.used_before(p) + ITEMS * chunk + 2 * q + 2 - ITEMS)
                                for s in range(4 * q, 4 * q + 4):
                                    pool.indirect_dma_start(
                                        out=rows[:, s, :], out_offset=None, in_=L.table[:, :],
                                        in_offset=bass.IndirectOffsetOnAxis(ap=picks[:, s:s + 1], axis=0),
                                    ).then_inc(L.quad[q], 16)
                        fetch(L, p, m + 2)
                    after(pool, pool_turn, L.meta_in, 16 * L.fetches * (MACROS + 2) * (p + 1))

        @block.scalar
        def _(act):
            def copy(to, of, **k):
                return nc.scalar.activation(to, of, ACT.Copy, **k)

            def norm(t, count, to):
                act.wait_ge(var_ready, count + 1)
                nc.scalar.activation(scales[:, 0, :], spread[:, 0, :], ACT.Sqrt).then_inc(sd_ready, 1)
                after(act, act_turn, ln_ready, count + 1)
                for g in range(GB):
                    last = nc.scalar.activation(to(g), arena[:, ds(t * GW + g * P, P)], ACT.Relu,
                                                bias=spread[:, 1, g:g + 1], scale=scales[:, 1, g:g + 1])
                last.then_inc(normed, 1)

            with act.Fori(0, NBG) as t:
                after(act, act_turn, h_saved, t + 1)
                norm(t, t, lambda g: agg[:, ds(NB * P + (t % 2) * GW + g * P, P)])

            act.wait_ge(passes_ready, 1)
            passes = act.value_load(small_i[0:1, 2:3], min_val=1, max_val=NB)

            def copy_turned(L, p, macro):
                at = (macro % 2) * MACRO_ITEMS
                if L.n == 1:
                    act.wait_ge(L.turned, L.rounds * (L.preps_before(p) + macro) + 1)
                    act.wait_ge(L.meta_in, 16 * L.fetches * (p * (MACROS + 2) + macro + 1))
                    copy(ef_pair, raw_ef.rearrange("p k (b w) -> p b k w", b=16)).then_inc(L.paired, 1)
                for r in range(L.rounds):
                    after(act, act_turn, L.turned, L.rounds * (L.preps_before(p) + macro) + r + 2)
                    if r >= 2:
                        last = copy(ef_t[:, 8 * (r - 2):8 * (r - 1), ds(at, MACRO_ITEMS)],
                                    b_turn[:, :].rearrange("p (b q) -> p b q", b=8))
                    else:
                        tables = [[src_t[:, :, :], dst_t[:, :, :], w_edge[:, :, :] if L.n == 0 else y_edge[:, 0]],
                                  [y_edge[:, 1], y_edge[:, 2], y_edge[:, 3]]][r]
                        for i, table in enumerate(tables):
                            last = copy(table[:, :, ds(at, MACRO_ITEMS)],
                                        b_turn[:, P * i:P * (i + 1)].rearrange("p (k q) -> p k q", k=2))
                    last.then_inc(L.turned_out, 1)
                after(act, act_turn, L.turned_out, L.rounds * (L.preps_before(p) + macro + 1) + 1)

            def copy_picks(L, q, chunk):
                first = ITEMS * (chunk % (2 * CHUNKS)) + 2 * q
                copy(picks[:, 4 * q:4 * q + 4].rearrange("p (j k) -> p k j", k=2),
                     src_t[:, :, ds(first, 2)]).then_inc(L.picks_ready, 1)

            def scale_rows(L, p, j, item, col):
                act.wait_ge(L.mixed, p * NIT + FREE + item - 1)
                act.sem_inc(act_turn, 1)
                for k in range(2):
                    row = rows[:, 2 * j + k, :].rearrange("p (c u) -> p c u", u=MUL)
                    to = scaled[:, j % 2]
                    y = lambda c: y_edge[:, c, k, ds(col, 1)]
                    copy(to[:, 8 * k:8 * k + 4, :], row, scale=y(0))
                    for i in range(3):
                        last = copy(to[:, 8 * k + 5 + i:17 + 3 * k + i:11 - 5 * k, :], row[:, 0:2 + i:1 + i, :],
                                    scale=y(1 + i))
                last.then_inc(L.scaled, 1)

            def silu_hidden1(L, r, n_before):
                act.wait_ge(L.mlp, n_before + 1)
                nc.scalar.activation(
                    hid1.rearrange("p q (b e) -> p e b q", e=NE8)[:, 4 * r:4 * r + 4],
                    b_mlp[:, :].rearrange("p (e b q) -> p e b q", e=4, b=16), ACT.Silu,
                    bias=b1_col[:, 0:1]).then_inc(L.mlp_out, 1)

            def silu_hidden2(L, r, n_before):
                act.wait_ge(L.mlp, n_before + 1)
                nc.scalar.activation(
                    hid2[:, 4 * r:4 * r + 4, :], b_mlp[:, :].rearrange("p (q e) -> p q e", q=4), ACT.Silu,
                    bias=b2_col[:, 0:1]).then_inc(L.mlp_out, 1)

            for L in layers:
                act.sem_inc(L.turned_out, 1)
                if L.n == 1:
                    act.sem_inc(L.mlp_out, 1)
                through = L.used if L.n == 0 else L.mixed
                with act.Fori(0, passes) as p:
                    after(act, act_turn, through, L.used_before(p))
                    copy_turned(L, p, 0)
                    for q in range(QUADS):
                        copy_picks(L, q, 0)
                    if L.n == 1:
                        done = p * (3 + 4 * NCH)
                        silu_hidden1(L, 0, done)
                        silu_hidden1(L, 1, done + 1)
                        silu_hidden2(L, 0, done + 2)
                    with act.Fori(0, MACROS) as m:
                        after(act, act_turn, through, L.used_before(p) + m * MACRO_ITEMS)
                        copy_turned(L, p, m + 1)
                        with act.Fori(0, CHUNKS) as c:
                            chunk = m * CHUNKS + c
                            done = p * (3 + 4 * NCH) + 3 + 4 * chunk
                            for q in range(QUADS):
                                after(act, act_turn, L.quad[q], 64 * (p * NCH + chunk) + 64)
                                copy_picks(L, q, chunk + 1)
                                if L.n == 0:
                                    continue
                                for j in (2 * q, 2 * q + 1):
                                    scale_rows(L, p, j, chunk * ITEMS + j, ITEMS * (chunk % (2 * CHUNKS)) + j)
                                if q == 0:
                                    silu_hidden2(L, 1, done)
                                elif q < 3:
                                    silu_hidden1(L, q - 1, done + q)
                                else:
                                    silu_hidden2(L, 0, done + 3)
                    after(act, act_turn, L.picks_ready, QUADS * (NCH + 1) * (p + 1))

                if L.n == 0:
                    act.sem_inc(up_out, 1)
                    act.wait_ge(L.walked, 1)
                    with act.Fori(0, NBG) as t:
                        after(act, act_turn, lin_ready, t + 1)
                        copy(sums_st, agg[:, ds(t * GW, GW)]).then_inc(sums_in, 1)
                        after(act, act_turn, h_turned, t + 1)
                        norm(t, NBG + t, lambda g: h_st[:, g * P:(g + 1) * P])
                        act.wait_ge(up_saved, t + 1)
                        after(act, act_turn, up_ready, t + 2)
                        for h, (a, z) in enumerate(HALVES):
                            last = copy(up_st[:, a:z], bank[4 + h][:, 0:z - a], scale=INV_UP)
                        last.then_inc(up_out, 1)

            act.wait_ge(layers[1].walked, 1)
            with act.Fori(0, NBG) as t:
                after(act, act_turn, fin_ready, t + 1)
                copy(fin_sums, agg[:, ds(t * 2 * GW, 2 * GW)]).then_inc(fin_staged, 1)

        @block.vector
        def _(dve):
            v = nc.vector
            links = [0]

            def link(ins):
                links[0] += 1
                ins.then_inc(chain, 1)
                dve.wait_ge(chain, links[0])

            v.memset(arena[:, (NB - 1) * P:NB * P], 0.0).then_inc(x_zeroed, 1)
            v.memset(w_up[:, :], 0.0)
            v.memset(a1_blocks[:, :, :], 0.0)
            v.memset(a3_pair[:, :], 0.0)
            v.memset(a2_pair[:, :], 0.0).then_inc(w_zeroed, 1)
            v.memset(zeros[:, :], 0.0)
            v.memset(src_f[:, :], 0.0)
            v.memset(w_out[:, :, :], 0.0)
            v.memset(row_f[:, :], 0.0)
            link(v.memset(small[:, :], 0.0))
            dve.wait_ge(consts, 6)

            dve.wait_ge(order_in, 64)
            d1 = agg[0:R1, 0:C1].bitcast(i32)
            falls = agg[0:R1, C1 + 2 * P * C2:2 * C1 + 2 * P * C2 - 1]
            link(v.tensor_tensor(falls, d1[:, 0:C1 - 1], d1[:, 1:C1], ALU.is_gt))
            link(v.tensor_reduce(small[0:R1, 0:1], falls, axis=AX.X, op=ALU.max))
            link(v.tensor_tensor(small[0:R1 - 1, 1:2], d1[0:R1 - 1, C1 - 1:C1], small_i[0:R1 - 1, 0:1], ALU.is_gt))
            d2 = agg[0:R2, C1:C1 + 2 * P * C2].bitcast(i32).rearrange("r (c e) -> r c e", e=2 * P)
            first_node = hot[:, 0, 0, 0:NB - 1]
            ends = hot[:, 0, 1, 0:C2]
            before = [hot[:, 1, 0, 0:NB - 1], hot[:, 1, 1, 0:NB - 1]]
            link(v.tensor_copy(ends[0:R2], d2[:, :, 2 * P - 1]))
            link(v.memset(before[1], 0.0))
            for c in range(C2):
                link(v.scalar_tensor_tensor(out=before[c % 2][0:R2], in0=first_node[0:R2], scalar=ends[0:R2, c:c + 1],
                                            in1=before[(c + 1) % 2][0:R2], op0=ALU.is_gt, op1=ALU.add))
            dve.sem_inc(votes, 1)
            dve.wait_ge(counted, 3)
            link(v.tensor_reduce(flag[:, 1:2], bank[0][:, 0:2], axis=AX.X, op=ALU.add))
            link(v.tensor_scalar(flag[:, 0:1], flag[:, 1:2], 1.0, None, ALU.min))
            link(v.tensor_scalar(flag[:, 1:2], flag[:, 0:1], -1.0, 1.0, ALU.mult, ALU.add))
            starts = before[C2 % 2]
            link(v.scalar_tensor_tensor(out=starts, in0=first_node, scalar=1.0 / P, in1=bank[1][:, 0:NB - 1],
                                        op0=ALU.mult, op1=ALU.add))
            link(v.tensor_scalar(small_i[:, 0:1], small_i[:, 1:2], MACRO_ITEMS - 1, None, ALU.bitwise_and))
            link(v.tensor_copy(small[:, 2:3], small_i[:, 0:1]))
            link(v.tensor_scalar(small[:, 3:4], small[:, 2:3], 0.0, None, ALU.mult))
            link(v.tensor_copy(small[:, 4:5], small_i[:, 1:2]))
            link(v.tensor_scalar(small[:, 3:4], small[:, 4:5], float(MACRO_ITEMS), None, ALU.is_ge))
            link(v.tensor_scalar(item_of[:, :], item_of[:, :], small[:, 2:3], None, ALU.add))
            for c in range(COLS):
                last = v.tensor_scalar(started[:, c, :], starts, item_of[:, c:c + 1], None, ALU.is_le)
            link(last)
            link(v.tensor_reduce(block_of[:, :], started, axis=AX.X, op=ALU.add))
            link(v.tensor_scalar(block_of[:, :], block_of[:, :], flag[:, 1:2], None, ALU.mult))
            v.tensor_copy(src_f[:, 0:COLS], block_of[:, :]).then_inc(votes, 1)
            link(v.tensor_tensor(tile_f[:, :], item_of[:, :], block_of[:, :], ALU.subtract))
            link(v.tensor_scalar(late[:, :], tile_f[:, :], 2.0, 1.0, ALU.mult, ALU.add))
            link(v.tensor_scalar(tile_odd_i[:, :], late[:, :], float(TILES - 1), None, ALU.min))
            link(v.tensor_scalar(tile_f[:, :], tile_f[:, :], 2.0, None, ALU.mult))
            link(v.tensor_scalar(tile_f[:, :], tile_f[:, :], small[:, 3:4], None, ALU.add))
            link(v.tensor_scalar(tile_i[:, :], tile_f[:, :], float(TILES - 1), None, ALU.min))
            link(v.tensor_scalar(late[:, :], tile_f[:, :], float(TILES - 1) + 0.5, NOWHERE, ALU.is_gt, ALU.mult))
            link(v.tensor_scalar(flag[:, 2:3], flag[:, 0:1], float(NB - 1), 1.0, ALU.mult, ALU.add))
            v.tensor_copy(small_i[:, 2:3], flag[:, 2:3]).then_inc(passes_ready, 1)
            dve.wait_ge(counted, 4)
            v.tensor_copy(agg[0:COLS, 0:MACRO_ITEMS], bank[2][0:COLS, 0:MACRO_ITEMS]).then_inc(plan_out, 1)
            v.tensor_copy(w_t[:, :], bank[3][:, 0:P])
            dve.wait_ge(w_in, 16 * len(loads))
            v.tensor_copy(w_out[0:MUL, 0, 0:MUL], raw_w[0:MUL, 0:MUL])
            v.tensor_scalar(w_out[0:MUL, 1, 0:MUL], raw_w[0:MUL, MUL:2 * MUL], INV_R3, None, ALU.mult)
            for i in range(3):
                lo = MUL * (i + 1)
                last = v.tensor_copy(w_out[lo:lo + MUL, :, MUL + i:MUL + i + 3 * MUL - 2:3],
                                     raw_w[lo:lo + MUL, 0:2 * MUL].rearrange("p (k w) -> p k w", k=2))
            link(last)
            dve.wait_ge(plan_in, 16)
            dve.wait_ge(passes_ready, 1)
            passes = dve.value_load(small_i[0:1, 2:3], min_val=1, max_val=NB)

            def layer_norm(t, count):
                for g in range(GB):
                    last = v.bn_stats(stats[:, g, :], arena[:, ds(t * GW + g * P, P)])
                last.then_inc(stats_done, 1)
                after(dve, dve_turn, stats_done, 3 * count + 1)
                for g in range(GB):
                    last = v.bn_aggr(moments[:, g, :], stats[:, g, :])
                last.then_inc(stats_done, 1)
                dve.wait_ge(normed, count + 1)
                dve.wait_ge(stats_done, 3 * count + 2)
                v.tensor_scalar(spread[:, 0, :], moments[:, :, 1], EPS, None, ALU.add).then_inc(var_ready, 1)
                dve.wait_ge(sd_ready, count + 1)
                v.reciprocal(scales[:, 1, :], scales[:, 0, :]).then_inc(stats_done, 1)
                dve.wait_ge(stats_done, 3 * count + 3)
                v.scalar_tensor_tensor(out=spread[:, 1, :], in0=moments[:, :, 0], scalar=-1.0, in1=scales[:, 1, :],
                                       op0=ALU.mult, op1=ALU.mult).then_inc(ln_ready, 1)

            dve.sem_inc(normed, 1)
            dve.wait_ge(x_in, 32)
            with dve.Fori(0, NBG) as t:
                layer_norm(t, t)

            def floats(L, p, macro):
                prep = L.preps_before(p) + macro
                dve.wait_ge(L.turned, L.rounds * prep + 1)
                after(dve, dve_turn, L.meta_in, 16 * L.fetches * (p * (MACROS + 2) + macro + 1))
                v.tensor_copy(src_f[:, :], raw_src[:, :])
                v.tensor_scalar(dst_f[:, :], raw_dst[:, :], shift[:, ds(macro, 1)], None, ALU.add).then_inc(L.floats, 1)

            def add_sums(L, p, item, a):
                width = P * (L.n + 1)
                at = dve.value_load(row_i[0:1, ds(item, 1)], min_val=0, max_val=NB - 1)
                dve.wait_ge(L.sums, L.sums_before(p) + item + 1)
                dve.wait_ge(L.added, p * (NIT + 1) + item + 1)
                v.tensor_tensor(agg[:, ds(at * width, width)], bank[4 + a][:, 0:width],
                                agg[:, ds(at * width, width)], ALU.add).then_inc(L.added, 1)

            for L in layers:
                if L.n == 1:
                    dve.sem_inc(L.mixed, FREE)
                    dve.wait_ge(table_ready, 2)
                link(v.memset(flag[:, 3:4], 0.0))
                v.memset(agg[:, 0:NB * P * (L.n + 1)], 0.0).then_inc(L.added, 1)
                with dve.Fori(0, passes) as p:
                    v.tensor_scalar(row_i[:, :], row_f[:, :], flag[0:1, 3:4], None, ALU.add)
                    v.tensor_scalar(shift[:, :], block_of[:, :], flag[:, 3:4], None, ALU.add).then_inc(L.plan_step, 1)
                    dve.wait_ge(L.plan_step, 2 * p + 1)
                    v.scalar_tensor_tensor(out=shift[:, :], in0=shift[:, :], scalar=-float(P), in1=late[:, :],
                                           op0=ALU.mult, op1=ALU.add).then_inc(L.plan, 1)
                    dve.wait_ge(L.plan, p + 1)
                    v.tensor_tensor(flag[:, 3:4], flag[:, 3:4], flag[:, 0:1], ALU.add).then_inc(L.plan_step, 1)
                    floats(L, p, 0)
                    with dve.Fori(0, MACROS) as m:
                        floats(L, p, m + 1)
                        after(dve, dve_turn, L.turned_out, L.rounds * (L.preps_before(p) + m + 1) + 1)
                        with dve.Fori(0, CHUNKS) as c:
                            chunk = m * CHUNKS + c
                            for j in range(ITEMS):
                                a = j % 2
                                item = chunk * ITEMS + j
                                col = ITEMS * (chunk % (2 * CHUNKS)) + j
                                for k in range(2):
                                    node = dst_t[:, k, ds(col, 1)]
                                    if L.n == 0:
                                        last = v.tensor_scalar(hot[:, a, k, :], iota_free[:, :], node,
                                                               w_edge[:, k, ds(col, 1)], ALU.is_equal, ALU.mult)
                                    else:
                                        v.tensor_scalar(hot[:, a, k, :], iota_free[:, :], node, None, ALU.is_equal)
                                if L.n == 0:
                                    last.then_inc(L.hot_ready, 1)
                                    add_sums(L, p, item, 1 - a)
                                    continue
                                dve.wait_ge(L.scaled, L.used_before(p) + item + 1)
                                to = scaled[:, a]
                                v.tensor_reduce(to[:, 4:16:8, :],
                                                to[:, 16:22, :].rearrange("p (k i) u -> p k u i", k=2),
                                                axis=AX.X, op=ALU.add).then_inc(L.dots, 1)
                                dve.wait_ge(L.weights, p * (NIT + 1) + item + 1)
                                four = to[:, 0:16, :].rearrange("p (r c) u -> p r c u", r=4)
                                wts = b_w[a][:, 0:2 * P].rearrange("p (g r u) -> p g r u", g=2, r=4)
                                v.tensor_tensor(msg[:, a, :, 1:4, :], four[:, :, 1:4, :],
                                                wts[:, 0].unsqueeze(2).to_broadcast([P, 4, 3, MUL]), ALU.mult)
                                dve.wait_ge(L.dots, p * NIT + item + 1)
                                v.tensor_tensor(msg[:, a, :, 0, :], four[:, :, 0, :], wts[:, 1], ALU.mult
                                                ).then_inc(L.mixed, 1)
                                add_sums(L, p, item, 1 - a)
                    add_sums(L, p, NIT, 1)
                    dve.wait_ge(L.plan_step, 2 * p + 2)
                dve.wait_ge(L.added, 1 + (NIT + 1) * passes)
                dve.sem_inc(L.walked, 3)

                if L.n == 0:
                    dve.sem_inc(x1_ready, 1)
                    dve.sem_inc(h_copied, 1)
                    with dve.Fori(0, NBG) as t:
                        dve.wait_ge(lin_ready, t + 2)
                        for h, (a, z) in enumerate(HALVES):
                            last = v.tensor_tensor(arena[:, ds(t * GW + a, z - a)], bank[h][:, 0:z - a],
                                                   arena[:, ds(t * GW + a, z - a)], ALU.add)
                        last.then_inc(x1_ready, 1)
                        after(dve, dve_turn, x1_ready, t + 2)
                        layer_norm(t, NBG + t)
                        dve.wait_ge(up_ready, t + 1)
                        dve.wait_ge(h_turned, t + 2)
                        for h, (a, z) in enumerate(HALVES):
                            last = v.tensor_copy(h_turn[:, a:z], bank[2 + h][:, 0:z - a])
                        last.then_inc(h_copied, 1)

            dve.sem_inc(fin_out, 1)
            with dve.Fori(0, NBG) as t:
                dve.wait_ge(fin_saved, t + 1)
                dve.wait_ge(fin_x, 16 * t + 16)
                dve.wait_ge(fin_ready, t + 2)
                for h, (a, z) in enumerate(HALVES):
                    last = v.scalar_tensor_tensor(out=fin_st[:, a:z], in0=bank[h][:, 0:z - a], scalar=INV_OUT,
                                                  in1=fin_x1[:, a:z], op0=ALU.mult, op1=ALU.add)
                last.then_inc(fin_out, 1)

        @block.tensor
        def _(pe):
            mm = nc.tensor.matmul
            pe.wait_ge(votes, 1)
            mm(bank[0][:, 0:2], ones[0:R1, :], small[0:R1, 0:2], start=True, stop=True).then_inc(counted, 1)
            total = hot[:, 1, (C2 - 1) % 2, 0:NB - 1]
            mm(bank[1][:, 0:NB - 1], ones[0:R2, :], total[0:R2, :], start=True, stop=True).then_inc(counted, 1)
            nc.tensor.transpose(bank[3][:, 0:P], w_t[:, :], ident[:, :]).then_inc(counted, 1)
            pe.wait_ge(votes, 2)
            nc.tensor.transpose(bank[2][:, 0:P], src_f[:, :], ident[:, :]).then_inc(counted, 1)
            pe.wait_ge(passes_ready, 1)
            passes = pe.value_load(small_i[0:1, 2:3], min_val=1, max_val=NB)

            def turn(L, p, macro):
                prep = L.preps_before(p) + macro
                after(pe, pe_turn, L.floats, prep + 1)
                if L.n == 1:
                    after(pe, pe_turn, L.paired, prep + 1)
                for r in range(L.rounds):
                    after(pe, pe_turn, L.turned_out, L.rounds * prep + r + 1)
                    if r >= 2:
                        for i in range(8):
                            e = 8 * (r - 2) + i
                            last = nc.tensor.transpose(b_turn[:, 64 * i:64 * i + 64], ef_pair[:, e, :, :].rearrange("p k w -> p (k w)"),
                                                       ident[0:64, 0:64])
                    else:
                        y = raw_ea.rearrange("p (e c) -> p c e", c=4)
                        of = [[src_f[:, :], dst_f[:, :], raw_w[:, :] if L.n == 0 else y[:, 0, :]],
                              [y[:, 1, :], y[:, 2, :], y[:, 3, :]]][r]
                        for i, rows_in in enumerate(of):
                            last = nc.tensor.transpose(b_turn[:, P * i:P * (i + 1)], rows_in, ident[:, :])
                    last.then_inc(L.turned, 1)

            def hidden1(L, p, macro, r, chunk, n_before):
                pe.wait_ge(L.turned_out, L.rounds * (L.preps_before(p) + macro + 1) + 1)
                pe.wait_ge(L.mlp_out, n_before + 1)
                col = ITEMS * (chunk % (2 * CHUNKS))
                for e in range(4):
                    last = mm(b_mlp[:, P * e:P * (e + 1)], a1_blocks[:, 4 * r + e, :], ef_t[:, :, ds(col, ITEMS)],
                              start=True, stop=True)
                last.then_inc(L.mlp, 1)

            def hidden2(L, r, n_before):
                pe.wait_ge(L.mlp_out, n_before + 1)
                mm(b_mlp[:, :], a2_pair[:, :], hid1[:, 4 * r:4 * r + 4, :].rearrange("p q e -> p (q e)"),
                   start=True, stop=True).then_inc(L.mlp, 1)

            def edge_weights(L, p, j, item):
                pe.wait_ge(L.mixed, p * NIT + FREE + item - 1)
                mm(b_w[j % 2][:, 0:2 * P], hid2[:, j, :], a3_pair[:, :], start=True, stop=True).then_inc(L.weights, 1)

            for L in layers:
                with pe.Fori(0, passes) as p:
                    pe.wait_ge(L.plan, p + 1)
                    mm(bank[5][:, 0:2 * P], zeros[:, :], a1_blocks[:, 0:2, :].rearrange("p e h -> p (e h)"),
                       start=True, stop=True).then_inc(L.sums, 1)
                    turn(L, p, 0)
                    if L.n == 1:
                        done = p * (3 + 4 * NCH)
                        hidden1(L, p, 0, 0, 0, done)
                        hidden1(L, p, 0, 1, 0, done + 1)
                        hidden2(L, 0, done + 2)
                        pe.wait_ge(L.mlp_out, done + 4)
                        edge_weights(L, p, 0, 0)
                    with pe.Fori(0, MACROS) as m:
                        turn(L, p, m + 1)
                        with pe.Fori(0, CHUNKS) as c:
                            chunk = m * CHUNKS + c
                            done = p * (3 + 4 * NCH) + 3 + 4 * chunk
                            if L.n == 1:
                                hidden2(L, 1, done)
                            for j in range(ITEMS):
                                a = j % 2
                                item = chunk * ITEMS + j
                                if L.n == 1:
                                    if j == 3:
                                        pe.wait_ge(L.mlp_out, done + 2)
                                    if j == ITEMS - 1:
                                        pe.wait_ge(L.mlp_out, done + 5)
                                    edge_weights(L, p, (j + 1) % ITEMS, item + 1)
                                if L.n == 0 and j % 2 == 0:
                                    pe.wait_ge(L.quad[j // 2], 64 * (p * NCH + chunk) + 64)
                                if L.n == 0:
                                    pe.wait_ge(L.hot_ready, p * NIT + item + 1)
                                else:
                                    pe.wait_ge(L.mixed, p * NIT + FREE + item + 1)
                                for half in range(L.n + 1):
                                    for k in range(2):
                                        of = rows[:, 2 * j + k, :] if L.n == 0 else \
                                            msg[:, a, 2 * k + half, :, :].rearrange("p c u -> p (c u)")
                                        last = mm(bank[4 + a][:, P * half:P * (half + 1)], of, hot[:, a, k, :],
                                                  start=k == 0, stop=k == 1)
                                last.then_inc(L.sums, 1)
                                if L.n == 1 and j in (0, 2):
                                    hidden1(L, p, m + 1, j // 2, chunk + 1, done + 1 + j // 2)
                                if L.n == 1 and j == 4:
                                    hidden2(L, 0, done + 3)

                if L.n == 0:
                    pe.sem_inc(lin_ready, 1)
                    pe.sem_inc(h_turned, 1)
                    pe.sem_inc(up_ready, 1)
                    with pe.Fori(0, NBG) as t:
                        pe.wait_ge(x1_ready, t + 1)
                        pe.wait_ge(sums_in, t + 1)
                        for g in range(GB):
                            h, at = where(g)
                            mm(bank[h][:, at:at + P], sums_st[:, g * P:(g + 1) * P], w_t[:, :], start=True, stop=False)
                            last = mm(bank[h][:, at:at + P], ones[0:1, :], bias_row[0:1, :], start=False, stop=True)
                        last.then_inc(lin_ready, 1)
                        pe.wait_ge(h_copied, t + 1)
                        pe.wait_ge(normed, NBG + t + 2)
                        for g in range(GB):
                            h, at = where(g)
                            last = nc.tensor.transpose(bank[2 + h][:, at:at + P], h_st[:, g * P:(g + 1) * P], ident[:, :])
                        last.then_inc(h_turned, 1)
                        pe.wait_ge(up_out, t + 1)
                        pe.wait_ge(h_copied, t + 2)
                        for g in range(GB):
                            h, at = where(g)
                            last = mm(bank[4 + h][:, at:at + P], h_turn[:, g * P:(g + 1) * P], w_up[:, :],
                                      start=True, stop=True)
                        last.then_inc(up_ready, 1)

            pe.sem_inc(fin_ready, 1)
            with pe.Fori(0, NBG) as t:
                pe.wait_ge(fin_out, t + 1)
                pe.wait_ge(fin_staged, t + 1)
                for g in range(GB):
                    h, at = where(g)
                    for k in range(2):
                        last = mm(bank[h][:, at:at + P], fin_sums[:, (2 * g + k) * P:(2 * g + k + 1) * P], w_out[:, k, :],
                                  start=k == 0, stop=k == 1)
                last.then_inc(fin_ready, 1)


_INS = ['x', 'src', 'dst', 'edge_attr_4', 'edge_attr_8', 'edge_weight', 'L0_gnn_W', 'L0_gnn_b', 'L1_gnn_W_up_s',
        'L1_gnn_W_up_v', 'L1_gnn_A1', 'L1_gnn_b1', 'L1_gnn_A2', 'L1_gnn_b2', 'L1_gnn_A3', 'L1_gnn_W_out_s',
        'L1_gnn_W_out_v']


def kernel(**inputs):
    import numpy as _np
    import concourse.bacc as _bacc
    from concourse import mybir as _mybir
    from concourse.bass_utils import run_bass_kernel_spmd as _run

    nc = _bacc.Bacc("TRN2", target_bir_lowering=False, num_devices=1)
    arrays, args = {}, []
    for name in _INS:
        a = _np.ascontiguousarray(inputs[name])
        arrays[f"in_{name}_dram"] = a
        args.append(nc.dram_tensor(f"in_{name}_dram", a.shape, _mybir.dt.from_np(a.dtype), kind="ExternalInput").ap())
    shape = inputs['x'].shape
    args.append(nc.dram_tensor("out_0_dram", shape, _mybir.dt.float32, kind="ExternalOutput").ap())
    build_gnn(nc, *args)
    r = _run(nc, [arrays], core_ids=[0])
    return r.results[0]["out_0_dram"]
```

```python
import math

import concourse.bass as bass
from concourse import mybir
from contextlib import ExitStack

P = 128
SLOTS = 16
ITEMS = SLOTS // 2
QUADS = SLOTS // 4
CHUNKS = 8
MACRO_ITEMS = CHUNKS * ITEMS
assert MACRO_ITEMS * 2 == P
MUL = 32
NE8 = 8


def divisor(n, most):
    return max(d for d in range(1, most + 1) if n % d == 0)


def build_gnn(nc, x, src, dst, ea4, ea8, ew, W, b, Wus, Wuv, A1, b1, A2, b2, A3, Wos, Wov, out):
    f32, i32 = mybir.dt.float32, mybir.dt.int32
    ALU, ACT, AX = mybir.AluOpType, mybir.ActivationFunctionType, mybir.AxisListType
    ds = bass.ds

    N, E = x.shape[0], src.shape[0]
    NB = -(-N // P)
    TAIL = N - (NB - 1) * P
    TILES = E // P
    assert E % P == 0 and x.shape[1] == P
    PAIRS = -(-TILES // 2)
    FULL = E // (2 * P)
    MACROS = -(-(PAIRS + NB - 1) // MACRO_ITEMS)
    COLS = MACROS + 2
    NCH = MACROS * CHUNKS
    NIT = MACROS * MACRO_ITEMS
    GB = divisor(NB, min(8, NB // 4))
    NBG = NB // GB
    GW = GB * P
    EPS = 1e-5
    INV_UP = 1.0 / math.sqrt(MUL)
    INV_OUT = 1.0 / math.sqrt(2 * MUL) / 10.0
    INV_R3 = 1.0 / math.sqrt(3.0)
    NOWHERE = 1.0e6
    R1 = divisor(E, P)
    C1 = E // R1
    R2 = divisor(FULL, P)
    C2 = FULL // R2
    ROW = NIT + 8
    TURN_AT, PAIR_AT, COPY_AT = [0, 2, 4, 6], [2, 4], [1, 3, 5, 7]
    LAG = 2
    FREE = ITEMS

    src_rows = src.rearrange("(t e) -> t e", e=P)
    dst_rows = dst.rearrange("(t e) -> t e", e=P)
    ew_rows = ew.rearrange("(t e) -> t e", e=P)
    ea4_rows = ea4.rearrange("(t e) c -> t (e c)", e=P)
    ea8_rows = ea8.rearrange("(t e) c -> t (e c)", e=P)

    h0_table = nc.dram_tensor("h0_table", (NB * P, P), f32, kind="Internal").ap()
    up_table = nc.dram_tensor("up_table", (NB * P, P), f32, kind="Internal").ap()
    x1_table = nc.dram_tensor("x1_table", (NB * P, P), f32, kind="Internal").ap()
    blocks_dram = nc.dram_tensor("blocks_dram", (COLS, MACRO_ITEMS), f32, kind="Internal").ap()

    with ExitStack() as ctx:
        def sb(name, shape, dt=f32):
            return ctx.enter_context(nc.sbuf_tensor(name, shape, dt))

        def sem(name):
            return ctx.enter_context(nc.semaphore(name))

        zeros = sb("zeros", [P, P])
        arena = sb("arena", [P, max(NB * P, 12160)])
        agg = sb("agg", [P, NB * 2 * P])
        ident = sb("ident", [P, P])
        ones = sb("ones", [P, P])
        iota_free = sb("iota_free", [P, P])
        w_t = sb("w_t", [P, P])
        bias_all = sb("bias_all", [P, P])
        w_up = sb("w_up", [P, P])
        a1_blocks = sb("a1_blocks", [P, NE8, P])
        a2_pair = sb("a2_pair", [P, P])
        a3_pair = sb("a3_pair", [P, 2 * P])
        b1_col = sb("b1_col", [P, 1])
        b2_col = sb("b2_col", [P, 1])
        w_out = sb("w_out", [P, 2, P])
        item_of = sb("item_of", [P, COLS])
        block_of = sb("block_of", [P, COLS])
        tile_f = sb("tile_f", [P, COLS])
        late = sb("late", [P, COLS])
        tile_i = sb("tile_i", [P, COLS], i32)
        tile_odd_i = sb("tile_odd_i", [P, COLS], i32)
        shift = sb("shift", [P, COLS])
        small = sb("small", [P, 24])
        small_i = sb("small_i", [P, 4], i32)
        flag = sb("flag", [P, 4])
        row_f = sb("row_f", [1, ROW])
        row_i = sb("row_i", [1, ROW], i32)
        stats = sb("stats", [P, GB, 6])
        moments = sb("moments", [P, GB, 2])
        spread = sb("spread", [P, GB])
        deviations = sb("deviations", [P, GB])
        scales = sb("scales", [P, 2, GB])
        meta_col = sb("meta_col", [P, 2], i32)
        raw_src = sb("raw_src", [P, P], i32)
        raw_dst = sb("raw_dst", [P, P], i32)
        raw_w = sb("raw_w", [P, P])
        src_f = sb("src_f", [P, P])
        dst_f = sb("dst_f", [P, P])
        src_t = sb("src_t", [P, 2, P])
        dst_t = sb("dst_t", [P, 2, P])
        w_edge = sb("w_edge", [P, 2, P])
        picks = sb("picks", [P, SLOTS], i32)
        rows = sb("rows", [P, SLOTS, P])
        hot = sb("hot", [P, 2, 2, P])

        place = [0]

        def part(width):
            place[0] += width
            assert place[0] <= arena.shape[1]
            return arena[:, place[0] - width:place[0]]

        raw_ea = part(4 * P)
        raw_ef = part(2 * NE8 * P).rearrange("p (k w) -> p k w", k=2)[0:64]
        ef_pair = part(2 * NE8 * P).rearrange("p (b k w) -> p b k w", b=16, k=2)[0:64]
        ef_t = part(16 * P).rearrange("p (b q) -> p b q", b=16)
        y_edge = part(4 * 2 * P).rearrange("p (c k q) -> p c k q", c=4, k=2)
        hid1 = part(ITEMS * P).rearrange("p (q e) -> p q e", q=ITEMS)
        hid2 = part(ITEMS * P).rearrange("p (q e) -> p q e", q=ITEMS)
        SP = 22
        scaled = part(2 * SP * MUL).rearrange("p (a c u) -> p a c u", a=2, c=SP)
        msg = part(2 * 4 * P).rearrange("p (a r c u) -> p a r c u", a=2, r=4, c=4)

        fin = arena[:, 20 * P:20 * P + 4 * GW]
        assert 4 * GW <= 32 * P
        fin_sums = rows[:, :, :].rearrange("p s d -> p (s d)")[:, 0:2 * GW]
        raw_w_out = rows[:, 0, :]
        spare = lambda i: agg[:, NB * P + i * GW:NB * P + (i + 1) * GW]
        sums_st, h_st, h_turn, up_st = (spare(i) for i in range(4))
        started = agg[:, NB * P:NB * P + COLS * (NB - 1)].rearrange("p (c b) -> p c b", c=COLS)
        HALVES = [(0, min(GW, 512)), (min(GW, 512), GW)]
        HALVES = [h for h in HALVES if h[1] > h[0]]
        NH = len(HALVES)
        blocks_in = lambda h: range(HALVES[h][0] // P, HALVES[h][1] // P)
        where = lambda g: (g * P // 512, g * P % 512)

        bank = [ctx.enter_context(nc.psum_tensor(f"bank{i}", [P, 512], f32)) for i in range(8)]
        b_w = [bank[0], bank[2]]
        b_sum = [bank[4], bank[5]]
        b_iota = bank[1][:, 0:P]
        b_mlp, b_turn = bank[6], bank[7]

        x_zeroed = sem("x_zeroed")
        x_in = sem("x_in")
        order_in = sem("order_in")
        w_zeroed = sem("w_zeroed")
        w_in = sem("w_in")
        w_set = sem("w_set")
        consts = sem("consts")
        votes = sem("votes")
        counted = sem("counted")
        chain = sem("chain")
        passes_ready = sem("passes_ready")
        plan_out = sem("plan_out"); plan_stored = sem("plan_stored"); plan_in = sem("plan_in")
        pool_turn = sem("pool_turn"); act_turn = sem("act_turn"); dve_turn = sem("dve_turn")
        pe_turn = sem("pe_turn"); sp_turn = sem("sp_turn")
        stats_done = sem("stats_done"); var_ready = sem("var_ready"); sd_ready = sem("sd_ready")
        ln_ready = sem("ln_ready")
        agg_zeroed = sem("agg_zeroed")
        biased = sem("biased")
        normed = sem("normed")
        h_stored = sem("h_stored"); h_saved = sem("h_saved")
        table_ready = sem("table_ready")
        sums_in = sem("sums_in")
        lin_ready = sem("lin_ready"); x1_ready = sem("x1_ready"); x1_stored = sem("x1_stored")
        h_turned = sem("h_turned"); h_copied = sem("h_copied")
        up_ready = sem("up_ready"); up_out = sem("up_out"); up_stored = sem("up_stored"); up_saved = sem("up_saved")
        fin_staged = sem("fin_staged"); fin_x = sem("fin_x"); fin_ready = sem("fin_ready")
        fin_out = sem("fin_out"); fin_stored = sem("fin_stored"); fin_saved = sem("fin_saved")

        class Layer:
            def __init__(self, n):
                s = lambda name: sem(f"{name}_{n}")
                self.n = n
                self.rounds = (1, 4)[n]
                self.fetches = (3, 5)[n]
                self.table = (h0_table, up_table)[n]
                self.plan = s("plan")
                self.plan_step = s("plan_step")
                self.col_ready = s("col_ready")
                self.meta_in = s("meta_in")
                self.floats = s("floats")
                self.turned = s("turned")
                self.turned_out = s("turned_out")
                self.picks_ready = s("picks_ready")
                self.quad = [s(f"quad{q}") for q in range(QUADS)]
                self.hot_ready = s("hot_ready")
                self.sums = s("sums")
                self.added = s("added")
                self.walked = s("walked")
                if n == 1:
                    self.paired = s("paired")
                    self.mlp = s("mlp")
                    self.mlp_out = s("mlp_out")
                    self.weights = s("weights")
                    self.scaled = s("scaled")
                    self.third = s("third")
                    self.dots = s("dots")
                    self.mixed = s("mixed")
                self.used = self.sums if n == 0 else self.mixed

            def used_before(self, p):
                return p * (NIT + LAG) + LAG + FREE if self.n == 0 else p * NIT + FREE

            def sums_before(self, p):
                return p * (NIT + LAG) + (FREE if self.n == 0 else 0)

            def preps_before(self, p):
                return p * (MACROS + 1)

        layers = [Layer(0), Layer(1)]

        def after(eng, turn, semaphore, value):
            eng.wait_ge(semaphore, value)
            eng.sem_inc(turn, 1)

        loads = [(bias_all[:, :], b.rearrange("(a n) -> a n", a=1).to_broadcast([P, P])), (w_up[0:MUL, 0:MUL], Wus)]
        for i in range(3):
            loads.append((w_up[MUL + i:MUL + i + 3 * MUL - 2:3, MUL * (i + 1):MUL * (i + 2)], Wuv))
        for k in range(2):
            lo = 64 * k
            for e in range(NE8):
                loads.append((a1_blocks[lo + 8 * e:lo + 8 * e + 8, e, lo:lo + 64], A1))
            loads.append((a2_pair[lo:lo + 64, lo:lo + 64], A2))
            for at, w in ((2 * k, 2), (2 * k + 1, 1), (2 * k + 4, 0), (2 * k + 5, 3)):
                loads.append((a3_pair[lo:lo + 64, MUL * at:MUL * (at + 1)], A3[:, MUL * w:MUL * (w + 1)]))
            loads.append((b1_col[lo:lo + 64, :], b1.rearrange("(n a) -> n a", a=1)))
            loads.append((b2_col[lo:lo + 64, :], b2.rearrange("(n a) -> n a", a=1)))
            loads.append((raw_w_out[0:MUL, MUL * k:MUL * (k + 1)], Wos[MUL * k:MUL * (k + 1), :]))
            for i in range(3):
                loads.append((raw_w_out[MUL * (i + 1):MUL * (i + 2), MUL * k:MUL * (k + 1)],
                              Wov[MUL * (1 - k):MUL * (2 - k), :]))

        block = ctx.enter_context(nc.Block())

        @block.sync
        def _(sp):
            rows_of = lambda table, t: table[ds(t * GW, GW), :].rearrange("(b p) d -> p b d", p=P)
            cut = lambda ap: ap.rearrange("p (b d) -> p b d", d=P)
            sp.dma_start(agg[0:R1, 0:C1].bitcast(i32), dst.rearrange("(r c) -> r c", r=R1)).then_inc(order_in, 16)
            sp.dma_start(agg[0:R2, C1:C1 + 2 * P * C2].bitcast(i32),
                         dst[0:FULL * 2 * P].rearrange("(r c) -> r c", r=R2)).then_inc(order_in, 16)
            sp.dma_start(small_i[0:R1 - 1, 0:1], dst.rearrange("(r c) -> r c", r=R1)[1:R1, 0:1],
                         allow_slow_non_contiguous=True).then_inc(order_in, 16)
            sp.dma_start(w_t[:, :], W).then_inc(order_in, 16)
            sp.wait_ge(x_zeroed, 1)
            sp.dma_start(cut(arena[:, 0:(NB - 1) * P]),
                         x[0:(NB - 1) * P, :].rearrange("(b p) d -> p b d", p=P)).then_inc(x_in, 16)
            sp.dma_start(arena[0:TAIL, (NB - 1) * P:NB * P], x[(NB - 1) * P:N, :]).then_inc(x_in, 16)
            sp.wait_ge(w_zeroed, 1)
            for to, of in loads:
                sp.dma_start(to, of).then_inc(w_in, 16)
            sp.wait_ge(plan_out, 1)
            sp.dma_start(blocks_dram, agg[0:COLS, 0:MACRO_ITEMS]).then_inc(plan_stored, 16)
            sp.wait_ge(plan_stored, 16)
            sp.dma_start(row_f[0:1, LAG:NIT + LAG],
                         blocks_dram[0:MACROS, :].rearrange("(a m) q -> a (m q)", a=1)).then_inc(plan_in, 16)
            sp.sem_inc(h_saved, 2)
            with sp.Fori(0, NBG) as t:
                sp.wait_ge(normed, t + 2)
                sp.dma_start(rows_of(h0_table, t), cut(agg[:, ds(NB * P + (t % 2) * GW, GW)])).then_inc(h_stored, 16)
                after(sp, h_saved, h_stored, 16 * t + 16)
            sp.sem_inc(table_ready, 1)
            sp.sem_inc(up_saved, 1)
            with sp.Fori(0, NBG) as t:
                sp.wait_ge(x1_ready, t + 2)
                sp.dma_start(rows_of(x1_table, t), cut(arena[:, ds(t * GW, GW)])).then_inc(x1_stored, 16)
                sp.wait_ge(up_out, t + 2)
                sp.dma_start(rows_of(up_table, t), cut(up_st)).then_inc(up_stored, 16)
                after(sp, up_saved, up_stored, 16 * t + 16)
            sp.wait_ge(x1_stored, 16 * NBG)
            sp.sem_inc(table_ready, 1)
            sp.wait_ge(layers[1].walked, 1)
            fin_x1 = lambda t: fin[:, ds((t % 2) * GW, GW)]
            fin_st = lambda t: fin[:, ds(2 * GW + (t % 2) * GW, GW)]

            sp.dma_start(cut(fin_x1(0)), rows_of(x1_table, 0)).then_inc(fin_x, 16)
            with sp.Fori(0, NBG - 1) as t:
                after(sp, sp_turn, fin_x, 16 * t + 16)
                after(sp, sp_turn, fin_out, NH * t + NH)
                sp.dma_start(cut(fin_x1(t + 1)), rows_of(x1_table, t + 1)).then_inc(fin_x, 16)
                sp.wait_ge(fin_out, NH * t + 2 * NH)
                sp.dma_start(rows_of(out, t), cut(fin_st(t))).then_inc(fin_stored, 16)
                after(sp, fin_saved, fin_stored, 16 * t + 16)
            sp.wait_ge(fin_out, NH * NBG + NH)
            st = fin[:, 2 * GW + (NBG - 1) % 2 * GW:][:, 0:GW]
            last = (NBG - 1) * GW
            if GB > 1:
                sp.dma_start(out[last:last + GW - P, :].rearrange("(b p) d -> p b d", p=P),
                             cut(st[:, 0:GW - P])).then_inc(fin_stored, 16)
            sp.dma_start(out[last + GW - P:N, :], st[0:TAIL, GW - P:GW]).then_inc(fin_stored, 16)
            sp.wait_ge(fin_stored, 16 * (NBG - 1 + (2 if GB > 1 else 1)))

        @block.gpsimd
        def _(pool):
            nc.gpsimd.memset(ones[:, :], 1.0).then_inc(consts, 1)
            exact = dict(allow_small_or_imprecise_dtypes=True)
            nc.gpsimd.iota(iota_free[:, :], [[1, P]], base=0, channel_multiplier=0, **exact).then_inc(consts, 1)
            nc.gpsimd.iota(item_of[:, :], [[MACRO_ITEMS, COLS]], base=0, channel_multiplier=0, **exact).then_inc(consts, 1)
            nc.gpsimd.iota(small_i[:, 1:2], [[1, 1]], base=0, channel_multiplier=1).then_inc(consts, 1)
            nc.gpsimd.iota(hot[:, 0, 0, 0:NB - 1], [[P, NB - 1]], base=P, channel_multiplier=0, **exact).then_inc(consts, 1)
            pool.wait_ge(consts, 5)
            nc.gpsimd.affine_select(out=ident[:, :], in_=ones[:, :], compare_op=ALU.is_equal, fill=0.0,
                                    base=0, pattern=[[-1, P]], channel_multiplier=1).then_inc(consts, 1)
            pool.wait_ge(passes_ready, 1)
            passes = pool.value_load(small_i[0:1, 2:3], min_val=1, max_val=NB)

            def fetch(L, p, macro):
                after(pool, pool_turn, L.turned, L.rounds * (L.preps_before(p) + macro) + 1)
                nc.gpsimd.tensor_copy(meta_col[:, 0:1], tile_i[:, ds(macro, 1)]).then_inc(L.col_ready, 1)
                nc.gpsimd.tensor_copy(meta_col[:, 1:2], tile_odd_i[:, ds(macro, 1)]).then_inc(L.col_ready, 1)
                after(pool, pool_turn, L.col_ready, 2 * (p * (MACROS + 2) + macro) + 2)
                every = [(raw_src[:, :], src_rows, P, 0), (raw_dst[:, :], dst_rows, P, 0)]
                if L.n == 0:
                    every += [(raw_w[:, :], ew_rows, P, 0)]
                else:
                    every += [(raw_ea, ea4_rows, P, 0), (raw_ef[:, 0, :], ea8_rows, 64, 0),
                              (raw_ef[:, 1, :], ea8_rows, 64, 1)]
                for to, of, parts, col in every:
                    pool.indirect_dma_start(
                        out=to, out_offset=None, in_=of,
                        in_offset=bass.IndirectOffsetOnAxis(ap=meta_col[0:parts, col:col + 1], axis=0),
                    ).then_inc(L.meta_in, 16)

            pool.wait_ge(layers[0].plan, 1)
            nc.gpsimd.memset(agg[:, 0:NB * P], 0.0).then_inc(agg_zeroed, 1)
            pool.wait_ge(w_in, 16 * len(loads))
            with pool.Fori(0, NBG) as t:
                after(pool, pool_turn, normed, t + 2)
                x_step = arena[:, ds(t * GW, GW)].rearrange("p (b d) -> p b d", d=P)
                nc.gpsimd.tensor_tensor(x_step, x_step, bias_all[:, :].unsqueeze(1).to_broadcast([P, GB, P]),
                                        ALU.add).then_inc(biased, 1)

            for L in layers:
                pool.sem_inc(L.turned, 1)
                pool.sem_inc(L.used, FREE)
                if L.n == 1:
                    pool.wait_ge(layers[0].walked, 1)
                    nc.gpsimd.memset(agg[:, NB * P + 4 * GW:2 * NB * P], 0.0).then_inc(agg_zeroed, 1)
                    with pool.Fori(0, NBG) as t:
                        after(pool, pool_turn, lin_ready, NH * t + 2 * NH)
                        nc.gpsimd.tensor_copy(agg[:, ds(t * GW, GW)].rearrange("p (b n) -> p b n", n=P),
                                              zeros[:, :].unsqueeze(1).to_broadcast([P, GB, P])).then_inc(agg_zeroed, 1)
                    pool.wait_ge(table_ready, 2)
                with pool.Fori(0, passes) as p:
                    after(pool, pool_turn, L.plan, p + 1)
                    fetch(L, p, 0)
                    fetch(L, p, 1)
                    after(pool, pool_turn, table_ready, L.n + 1)
                    after(pool, pool_turn, w_set, 1)
                    with pool.Fori(0, MACROS) as m:
                        with pool.Fori(0, CHUNKS) as c:
                            chunk = m * CHUNKS + c
                            for q in range(QUADS):
                                after(pool, pool_turn, L.picks_ready, QUADS * (p * (NCH + 1) + chunk) + q + 1)
                                after(pool, pool_turn, L.used,
                                      L.used_before(p) + ITEMS * chunk + 2 * q + 2 - ITEMS)
                                for s in range(4 * q, 4 * q + 4):
                                    pool.indirect_dma_start(
                                        out=rows[:, s, :], out_offset=None, in_=L.table[:, :],
                                        in_offset=bass.IndirectOffsetOnAxis(ap=picks[:, s:s + 1], axis=0),
                                    ).then_inc(L.quad[q], 16)
                        fetch(L, p, m + 2)
                    after(pool, pool_turn, L.meta_in, 16 * L.fetches * (MACROS + 2) * (p + 1))

        @block.scalar
        def _(act):
            def copy(to, of, **k):
                return nc.scalar.activation(to, of, ACT.Copy, **k)

            def deviation(count):
                act.wait_ge(var_ready, count + 1)
                nc.scalar.activation(deviations[:, :], spread[:, :], ACT.Sqrt).then_inc(sd_ready, 1)

            def norm(t, count, to):
                after(act, act_turn, ln_ready, count + 1)
                for g in range(GB):
                    last = nc.scalar.activation(to(g), arena[:, ds(t * GW + g * P, P)], ACT.Relu,
                                                bias=scales[:, 1, g:g + 1], scale=scales[:, 0, g:g + 1])
                last.then_inc(normed, 1)

            with act.Fori(0, NBG) as t:
                deviation(t)
                after(act, act_turn, h_saved, t + 1)
                norm(t, t, lambda g: agg[:, ds(NB * P + (t % 2) * GW + g * P, P)])

            act.wait_ge(passes_ready, 1)
            passes = act.value_load(small_i[0:1, 2:3], min_val=1, max_val=NB)

            def pair_features(L, p, macro, h):
                act.wait_ge(L.turned, L.rounds * (L.preps_before(p) + macro) + 1)
                act.wait_ge(L.meta_in, 16 * L.fetches * (p * (MACROS + 2) + macro + 1))
                copy(ef_pair[:, 8 * h:8 * h + 8],
                     raw_ef.rearrange("p k (b w) -> p b k w", b=16)[:, 8 * h:8 * h + 8]).then_inc(L.paired, 1)

            def copy_turned(L, p, macro, r):
                at = (macro % 2) * MACRO_ITEMS
                after(act, act_turn, L.turned, L.rounds * (L.preps_before(p) + macro) + r + 2)
                if r >= 2:
                    last = copy(ef_t[:, 8 * (r - 2):8 * (r - 1), ds(at, MACRO_ITEMS)],
                                b_turn[:, :].rearrange("p (b q) -> p b q", b=8))
                else:
                    tables = [[src_t[:, :, :], dst_t[:, :, :], w_edge[:, :, :] if L.n == 0 else y_edge[:, 0]],
                              [y_edge[:, 1], y_edge[:, 2], y_edge[:, 3]]][r]
                    for i, table in enumerate(tables):
                        last = copy(table[:, :, ds(at, MACRO_ITEMS)],
                                    b_turn[:, P * i:P * (i + 1)].rearrange("p (k q) -> p k q", k=2))
                last.then_inc(L.turned_out, 1)

            def tables_stand(L, p, macro):
                after(act, act_turn, L.turned_out, L.rounds * (L.preps_before(p) + macro + 1) + 1)

            def copy_picks(L, q, chunk):
                first = ITEMS * (chunk % (2 * CHUNKS)) + 2 * q
                copy(picks[:, 4 * q:4 * q + 4].rearrange("p (j k) -> p k j", k=2),
                     src_t[:, :, ds(first, 2)]).then_inc(L.picks_ready, 1)

            def scale_rows(L, p, j, item, col):
                act.wait_ge(L.mixed, p * NIT + FREE + item - 1)
                act.sem_inc(act_turn, 1)
                for k in range(2):
                    row = rows[:, 2 * j + k, :].rearrange("p (c u) -> p c u", u=MUL)
                    to = scaled[:, j % 2]
                    y = lambda c: y_edge[:, c, k, ds(col, 1)]
                    copy(to[:, 8 * k:8 * k + 4, :], row, scale=y(0))
                    for i in range(2):
                        last = copy(to[:, 8 * k + 5 + i:17 + 3 * k + i:11 - 5 * k, :], row[:, 0:2 + i:1 + i, :],
                                    scale=y(1 + i))
                last.then_inc(L.scaled, 1)

            def silu_hidden1(L, r, n_before):
                act.wait_ge(L.mlp, n_before + 1)
                nc.scalar.activation(
                    hid1.rearrange("p q (b e) -> p e b q", e=NE8)[:, 4 * r:4 * r + 4],
                    b_mlp[:, :].rearrange("p (e b q) -> p e b q", e=4, b=16), ACT.Silu,
                    bias=b1_col[:, 0:1]).then_inc(L.mlp_out, 1)

            def silu_hidden2(L, r, n_before):
                act.wait_ge(L.mlp, n_before + 1)
                nc.scalar.activation(
                    hid2[:, 4 * r:4 * r + 4, :], b_mlp[:, :].rearrange("p (q e) -> p q e", q=4), ACT.Silu,
                    bias=b2_col[:, 0:1]).then_inc(L.mlp_out, 1)

            act.wait_ge(w_set, 1)
            for L in layers:
                act.sem_inc(L.turned_out, 1)
                if L.n == 1:
                    act.sem_inc(L.mlp_out, 1)
                with act.Fori(0, passes) as p:
                    after(act, act_turn, L.used, L.used_before(p))
                    if L.n == 1:
                        for h in range(2):
                            pair_features(L, p, 0, h)
                    for r in range(L.rounds):
                        copy_turned(L, p, 0, r)
                    tables_stand(L, p, 0)
                    for q in range(QUADS):
                        copy_picks(L, q, 0)
                    if L.n == 1:
                        done = p * (3 + 4 * NCH)
                        silu_hidden1(L, 0, done)
                        silu_hidden1(L, 1, done + 1)
                        silu_hidden2(L, 0, done + 2)

                    def walk_chunk(m, c):
                        chunk = m * CHUNKS + c
                        done = p * (3 + 4 * NCH) + 3 + 4 * chunk
                        first = isinstance(c, int)
                        for q in range(QUADS):
                            after(act, act_turn, L.quad[q], 64 * (p * NCH + chunk) + 64)
                            copy_picks(L, q, chunk + 1)
                            if L.n == 0:
                                continue
                            for j in (2 * q, 2 * q + 1):
                                scale_rows(L, p, j, chunk * ITEMS + j, ITEMS * (chunk % (2 * CHUNKS)) + j)
                                if first and j in PAIR_AT:
                                    pair_features(L, p, m + 1, PAIR_AT.index(j))
                                if first and j in COPY_AT:
                                    copy_turned(L, p, m + 1, COPY_AT.index(j))
                            if q == 0:
                                silu_hidden2(L, 1, done)
                            elif q < 3:
                                silu_hidden1(L, q - 1, done + q)
                            else:
                                silu_hidden2(L, 0, done + 3)

                    with act.Fori(0, MACROS) as m:
                        if L.n == 0:
                            after(act, act_turn, L.used, L.used_before(p) + m * MACRO_ITEMS)
                            copy_turned(L, p, m + 1, 0)
                        walk_chunk(m, 0)
                        tables_stand(L, p, m + 1)
                        with act.Fori(1, CHUNKS) as c:
                            walk_chunk(m, c)
                    after(act, act_turn, L.picks_ready, QUADS * (NCH + 1) * (p + 1))

                if L.n == 0:
                    act.sem_inc(up_out, 1)
                    act.wait_ge(L.walked, 1)

                    def stage_sums(t):
                        for h, (a, z) in enumerate(HALVES):
                            after(act, act_turn, lin_ready, NH * t + h + 1)
                            copy(sums_st[:, a:z], agg[:, ds(t * GW + a, z - a)]).then_inc(sums_in, 1)

                    def norm_step(t):
                        after(act, act_turn, h_turned, t + 1)
                        norm(t, NBG + t, lambda g: h_st[:, g * P:(g + 1) * P])

                    def table_step(t):
                        act.wait_ge(up_saved, t + 1)
                        after(act, act_turn, up_ready, t + 2)
                        for h, (a, z) in enumerate(HALVES):
                            last = copy(up_st[:, a:z], bank[4 + h][:, 0:z - a], scale=INV_UP)
                        last.then_inc(up_out, 1)

                    stage_sums(0)
                    stage_sums(1)
                    deviation(NBG)
                    with act.Fori(0, NBG - 2) as t:
                        norm_step(t)
                        stage_sums(t + 2)
                        deviation(NBG + t + 1)
                        table_step(t)
                    norm_step(NBG - 2)
                    deviation(2 * NBG - 1)
                    table_step(NBG - 2)
                    norm_step(NBG - 1)
                    table_step(NBG - 1)

            act.wait_ge(layers[1].walked, 1)
            with act.Fori(0, NBG) as t:
                for h, (a, z) in enumerate(HALVES):
                    after(act, act_turn, fin_ready, NH * t + h + 1)
                    copy(fin_sums[:, 2 * a:2 * z], agg[:, ds(t * 2 * GW + 2 * a, 2 * (z - a))]).then_inc(fin_staged, 1)

        @block.vector
        def _(dve):
            v = nc.vector
            links = [0]

            def link(ins):
                links[0] += 1
                ins.then_inc(chain, 1)
                dve.wait_ge(chain, links[0])

            v.memset(arena[:, (NB - 1) * P:NB * P], 0.0).then_inc(x_zeroed, 1)
            v.memset(w_up[:, :], 0.0)
            v.memset(a1_blocks[:, :, :], 0.0)
            v.memset(a3_pair[:, :], 0.0)
            v.memset(a2_pair[:, :], 0.0).then_inc(w_zeroed, 1)
            v.memset(zeros[:, :], 0.0)
            v.memset(src_f[:, :], 0.0)
            v.memset(w_out[:, :, :], 0.0)
            v.memset(row_f[:, :], 0.0)
            link(v.memset(small[:, :], 0.0))
            dve.wait_ge(consts, 6)

            dve.wait_ge(order_in, 64)
            d1 = agg[0:R1, 0:C1].bitcast(i32)
            falls = agg[0:R1, C1 + 2 * P * C2:2 * C1 + 2 * P * C2 - 1]
            link(v.tensor_tensor(falls, d1[:, 0:C1 - 1], d1[:, 1:C1], ALU.is_gt))
            link(v.tensor_reduce(small[0:R1, 0:1], falls, axis=AX.X, op=ALU.max))
            link(v.tensor_tensor(small[0:R1 - 1, 1:2], d1[0:R1 - 1, C1 - 1:C1], small_i[0:R1 - 1, 0:1], ALU.is_gt))
            d2 = agg[0:R2, C1:C1 + 2 * P * C2].bitcast(i32).rearrange("r (c e) -> r c e", e=2 * P)
            first_node = hot[:, 0, 0, 0:NB - 1]
            ends = hot[:, 0, 1, 0:C2]
            before = [hot[:, 1, 0, 0:NB - 1], hot[:, 1, 1, 0:NB - 1]]
            link(v.tensor_copy(ends[0:R2], d2[:, :, 2 * P - 1]))
            link(v.memset(before[1], 0.0))
            for c in range(C2):
                link(v.scalar_tensor_tensor(out=before[c % 2][0:R2], in0=first_node[0:R2], scalar=ends[0:R2, c:c + 1],
                                            in1=before[(c + 1) % 2][0:R2], op0=ALU.is_gt, op1=ALU.add))
            dve.sem_inc(votes, 1)
            dve.wait_ge(counted, 3)
            link(v.tensor_reduce(flag[:, 1:2], bank[0][:, 0:2], axis=AX.X, op=ALU.add))
            link(v.tensor_scalar(flag[:, 0:1], flag[:, 1:2], 1.0, None, ALU.min))
            link(v.tensor_scalar(flag[:, 1:2], flag[:, 0:1], -1.0, 1.0, ALU.mult, ALU.add))
            starts = before[C2 % 2]
            link(v.scalar_tensor_tensor(out=starts, in0=first_node, scalar=1.0 / P, in1=bank[1][:, 0:NB - 1],
                                        op0=ALU.mult, op1=ALU.add))
            link(v.tensor_scalar(small_i[:, 0:1], small_i[:, 1:2], MACRO_ITEMS - 1, None, ALU.bitwise_and))
            link(v.tensor_copy(small[:, 2:3], small_i[:, 0:1]))
            link(v.tensor_scalar(small[:, 3:4], small[:, 2:3], 0.0, None, ALU.mult))
            link(v.tensor_copy(small[:, 4:5], small_i[:, 1:2]))
            link(v.tensor_scalar(small[:, 3:4], small[:, 4:5], float(MACRO_ITEMS), None, ALU.is_ge))
            link(v.tensor_scalar(item_of[:, :], item_of[:, :], small[:, 2:3], None, ALU.add))
            for c in range(COLS):
                last = v.tensor_scalar(started[:, c, :], starts, item_of[:, c:c + 1], None, ALU.is_le)
            link(last)
            link(v.tensor_reduce(block_of[:, :], started, axis=AX.X, op=ALU.add))
            link(v.tensor_scalar(block_of[:, :], block_of[:, :], flag[:, 1:2], None, ALU.mult))
            v.tensor_copy(src_f[:, 0:COLS], block_of[:, :]).then_inc(votes, 1)
            link(v.tensor_tensor(tile_f[:, :], item_of[:, :], block_of[:, :], ALU.subtract))
            link(v.tensor_scalar(late[:, :], tile_f[:, :], 2.0, 1.0, ALU.mult, ALU.add))
            link(v.tensor_scalar(tile_odd_i[:, :], late[:, :], float(TILES - 1), None, ALU.min))
            link(v.tensor_scalar(tile_f[:, :], tile_f[:, :], 2.0, None, ALU.mult))
            link(v.tensor_scalar(tile_f[:, :], tile_f[:, :], small[:, 3:4], None, ALU.add))
            link(v.tensor_scalar(tile_i[:, :], tile_f[:, :], float(TILES - 1), None, ALU.min))
            link(v.tensor_scalar(late[:, :], tile_f[:, :], float(TILES - 1) + 0.5, NOWHERE, ALU.is_gt, ALU.mult))
            link(v.tensor_scalar(flag[:, 2:3], flag[:, 0:1], float(NB - 1), 1.0, ALU.mult, ALU.add))
            v.tensor_copy(small_i[:, 2:3], flag[:, 2:3]).then_inc(passes_ready, 1)
            dve.wait_ge(counted, 4)
            v.tensor_copy(agg[0:COLS, 0:MACRO_ITEMS], bank[2][0:COLS, 0:MACRO_ITEMS]).then_inc(plan_out, 1)
            v.tensor_copy(w_t[:, :], bank[3][:, 0:P])
            dve.wait_ge(plan_in, 16)
            dve.wait_ge(passes_ready, 1)
            passes = dve.value_load(small_i[0:1, 2:3], min_val=1, max_val=NB)

            def make_plan(L, p):
                if not isinstance(p, int):
                    dve.wait_ge(L.plan_step, 2 * p)
                v.tensor_scalar(row_i[:, :], row_f[:, :], flag[0:1, 3:4], None, ALU.add)
                v.tensor_scalar(shift[:, :], block_of[:, :], flag[:, 3:4], None, ALU.add).then_inc(L.plan_step, 1)
                dve.wait_ge(L.plan_step, 2 * p + 1)
                v.scalar_tensor_tensor(out=shift[:, :], in0=shift[:, :], scalar=-float(P), in1=late[:, :],
                                       op0=ALU.mult, op1=ALU.add).then_inc(L.plan, 1)
                dve.wait_ge(L.plan, p + 1)
                v.tensor_tensor(flag[:, 3:4], flag[:, 3:4], flag[:, 0:1], ALU.add).then_inc(L.plan_step, 1)

            link(v.memset(flag[:, 3:4], 0.0))
            make_plan(layers[0], 0)

            def row_stats(t, count):
                for g in range(GB):
                    last = v.bn_stats(stats[:, g, :], arena[:, ds(t * GW + g * P, P)])
                last.then_inc(stats_done, 1)
                after(dve, dve_turn, stats_done, 3 * count + 1)
                for g in range(GB):
                    last = v.bn_aggr(moments[:, g, :], stats[:, g, :])
                last.then_inc(stats_done, 1)
                dve.wait_ge(stats_done, 3 * count + 2)
                v.tensor_scalar(spread[:, :], moments[:, :, 1], EPS, None, ALU.add).then_inc(var_ready, 1)

            def row_scales(count):
                dve.wait_ge(normed, count + 1)
                dve.wait_ge(sd_ready, count + 1)
                v.reciprocal(scales[:, 0, :], deviations[:, :]).then_inc(stats_done, 1)
                dve.wait_ge(stats_done, 3 * count + 3)
                v.scalar_tensor_tensor(out=scales[:, 1, :], in0=moments[:, :, 0], scalar=-1.0, in1=scales[:, 0, :],
                                       op0=ALU.mult, op1=ALU.mult).then_inc(ln_ready, 1)

            dve.sem_inc(normed, 1)
            dve.wait_ge(x_in, 32)
            with dve.Fori(0, NBG) as t:
                row_stats(t, t)
                row_scales(t)

            dve.wait_ge(w_in, 16 * len(loads))
            v.tensor_copy(w_out[0:MUL, 0, 0:MUL], raw_w_out[0:MUL, 0:MUL])
            v.tensor_scalar(w_out[0:MUL, 1, 0:MUL], raw_w_out[0:MUL, MUL:2 * MUL], INV_R3, None, ALU.mult)
            for i in range(3):
                lo = MUL * (i + 1)
                last = v.tensor_copy(w_out[lo:lo + MUL, :, MUL + i:MUL + i + 3 * MUL - 2:3],
                                     raw_w_out[lo:lo + MUL, 0:2 * MUL].rearrange("p (k w) -> p k w", k=2))
            last.then_inc(w_set, 1)

            def floats(L, p, macro):
                prep = L.preps_before(p) + macro
                dve.wait_ge(L.turned, L.rounds * prep + 1)
                after(dve, dve_turn, L.meta_in, 16 * L.fetches * (p * (MACROS + 2) + macro + 1))
                v.tensor_copy(src_f[:, :], raw_src[:, :])
                v.tensor_scalar(dst_f[:, :], raw_dst[:, :], shift[:, ds(macro, 1)], None, ALU.add).then_inc(L.floats, 1)

            def block_at(item):
                return dve.value_load(row_i[0:1, ds(item, 1)], min_val=0, max_val=NB - 1)

            def add_sums(L, p, item, a, at):
                width = P * (L.n + 1)
                if L.n == 0:
                    dve.wait_ge(L.sums, L.sums_before(p) + item + 1)
                dve.wait_ge(L.added, p * (NIT + LAG) + item + 1)
                v.tensor_tensor(agg[:, ds(at * width, width)], bank[4 + a][:, 0:width],
                                agg[:, ds(at * width, width)], ALU.add).then_inc(L.added, 1)

            for L in layers:
                if L.n == 0:
                    dve.wait_ge(agg_zeroed, 1)
                    dve.sem_inc(L.added, 1)
                else:
                    link(v.memset(flag[:, 3:4], 0.0))
                    make_plan(L, 0)
                    v.tensor_copy(b_iota, iota_free[:, :])
                    dve.wait_ge(table_ready, 2)
                    link(v.memset(agg[:, NB * P:NB * P + 4 * GW], 0.0))
                    dve.wait_ge(agg_zeroed, NBG + 2)
                    dve.sem_inc(L.added, 1)
                with dve.Fori(0, passes) as p:
                    floats(L, p, 0)
                    with dve.Fori(0, MACROS) as m:
                        floats(L, p, m + 1)
                        after(dve, dve_turn, L.turned_out, L.rounds * (L.preps_before(p) + m + 1) + 1)
                        with dve.Fori(0, CHUNKS) as c:
                            chunk = m * CHUNKS + c
                            for j in range(ITEMS):
                                a = j % 2
                                item = chunk * ITEMS + j
                                col = ITEMS * (chunk % (2 * CHUNKS)) + j
                                at = block_at(item)
                                if L.n == 0:
                                    add_sums(L, p, item, a, at)
                                    for k in range(2):
                                        last = v.tensor_scalar(hot[:, a, k, :], iota_free[:, :], dst_t[:, k, ds(col, 1)],
                                                               w_edge[:, k, ds(col, 1)], ALU.is_equal, ALU.mult)
                                    last.then_inc(L.hot_ready, 1)
                                    continue
                                if j % 2 == 0:
                                    dve.wait_ge(L.quad[j // 2], 64 * (p * NCH + chunk) + 64)
                                for k in range(2):
                                    row = rows[:, 2 * j + k, :].rearrange("p (c u) -> p c u", u=MUL)
                                    last = v.tensor_scalar(scaled[:, a, 8 * k + 7:19 + 3 * k:11 - 5 * k, :], row[:, 0:4:3, :],
                                                           y_edge[:, 3, k, ds(col, 1)], None, ALU.mult)
                                last.then_inc(L.third, 1)
                                dve.wait_ge(L.sums, L.sums_before(p) + item + 1)
                                v.tensor_tensor(hot[:, a, :, :], b_iota.unsqueeze(1).to_broadcast([P, 2, P]),
                                                dst_t[:, :, ds(col, 1)].to_broadcast([P, 2, P]), ALU.is_equal)
                                dve.wait_ge(L.third, p * NIT + item + 1)
                                dve.wait_ge(L.scaled, p * NIT + item + 1)
                                to = scaled[:, a]
                                v.tensor_reduce(to[:, 4:16:8, :],
                                                to[:, 16:22, :].rearrange("p (k i) u -> p k u i", k=2),
                                                axis=AX.X, op=ALU.add).then_inc(L.dots, 1)
                                add_sums(L, p, item, a, at)
                                dve.wait_ge(L.weights, p * (NIT + 1) + item + 1)
                                four = to[:, 0:16, :].rearrange("p (r c) u -> p r c u", r=4)
                                wts = b_w[a][:, 0:2 * P].rearrange("p (g r u) -> p g r u", g=2, r=4)
                                v.tensor_tensor(msg[:, a, :, 1:4, :], four[:, :, 1:4, :],
                                                wts[:, 0].unsqueeze(2).to_broadcast([P, 4, 3, MUL]), ALU.mult)
                                dve.wait_ge(L.dots, p * NIT + item + 1)
                                v.tensor_tensor(msg[:, a, :, 0, :], four[:, :, 0, :], wts[:, 1], ALU.mult
                                                ).then_inc(L.mixed, 1)
                    for a in range(LAG):
                        at = block_at(NIT + a)
                        if L.n == 1:
                            dve.wait_ge(L.sums, L.sums_before(p) + NIT + a + 1)
                        add_sums(L, p, NIT + a, a, at)
                    make_plan(L, p + 1)
                dve.wait_ge(L.plan_step, 2 * passes + 2)
                if L.n == 0:
                    dve.wait_ge(biased, NBG)
                dve.wait_ge(L.added, 1 + (NIT + LAG) * passes)
                dve.sem_inc(L.walked, 1)

                if L.n == 0:
                    dve.sem_inc(x1_ready, 1)
                    dve.sem_inc(h_copied, 1)

                    def add_x(t):
                        dve.wait_ge(lin_ready, NH * t + 2 * NH)
                        for h, (a, z) in enumerate(HALVES):
                            last = v.tensor_tensor(arena[:, ds(t * GW + a, z - a)], bank[h][:, 0:z - a],
                                                   arena[:, ds(t * GW + a, z - a)], ALU.add)
                        last.then_inc(x1_ready, 1)
                        after(dve, dve_turn, x1_ready, t + 2)

                    def copy_turned_rows(t):
                        dve.wait_ge(up_ready, t + 1)
                        dve.wait_ge(h_turned, t + 2)
                        for h, (a, z) in enumerate(HALVES):
                            last = v.tensor_copy(h_turn[:, a:z], bank[2 + h][:, 0:z - a])
                        last.then_inc(h_copied, 1)

                    add_x(0)
                    row_stats(0, NBG)
                    row_scales(NBG)
                    with dve.Fori(0, NBG - 1) as t:
                        add_x(t + 1)
                        copy_turned_rows(t)
                        row_stats(t + 1, NBG + t + 1)
                        row_scales(NBG + t + 1)
                    copy_turned_rows(NBG - 1)

            dve.sem_inc(fin_out, NH)
            dve.sem_inc(fin_saved, 2)
            with dve.Fori(0, NBG) as t:
                dve.wait_ge(fin_saved, t + 1)
                dve.wait_ge(fin_x, 16 * t + 16)
                for h, (a, z) in enumerate(HALVES):
                    dve.wait_ge(fin_ready, NH * t + NH + h + 1)
                    v.scalar_tensor_tensor(out=fin[:, ds(2 * GW + (t % 2) * GW + a, z - a)], in0=bank[h][:, 0:z - a],
                                           scalar=INV_OUT, in1=fin[:, ds((t % 2) * GW + a, z - a)], op0=ALU.mult,
                                           op1=ALU.add).then_inc(fin_out, 1)

        @block.tensor
        def _(pe):
            mm = nc.tensor.matmul
            pe.wait_ge(votes, 1)
            mm(bank[0][:, 0:2], ones[0:R1, :], small[0:R1, 0:2], start=True, stop=True).then_inc(counted, 1)
            total = hot[:, 1, (C2 - 1) % 2, 0:NB - 1]
            mm(bank[1][:, 0:NB - 1], ones[0:R2, :], total[0:R2, :], start=True, stop=True).then_inc(counted, 1)
            nc.tensor.transpose(bank[3][:, 0:P], w_t[:, :], ident[:, :]).then_inc(counted, 1)
            pe.wait_ge(votes, 2)
            nc.tensor.transpose(bank[2][:, 0:P], src_f[:, :], ident[:, :]).then_inc(counted, 1)
            pe.wait_ge(passes_ready, 1)
            passes = pe.value_load(small_i[0:1, 2:3], min_val=1, max_val=NB)

            pe.wait_ge(w_set, 1)

            def turn(L, p, macro, r):
                prep = L.preps_before(p) + macro
                after(pe, pe_turn, L.turned_out, L.rounds * prep + r + 1)
                if r >= 2:
                    after(pe, pe_turn, L.paired, 2 * prep + r - 1)
                    for i in range(8):
                        e = 8 * (r - 2) + i
                        last = nc.tensor.transpose(b_turn[:, 64 * i:64 * i + 64],
                                                   ef_pair[:, e, :, :].rearrange("p k w -> p (k w)"), ident[0:64, 0:64])
                else:
                    after(pe, pe_turn, L.floats, prep + 1)
                    y = raw_ea.rearrange("p (e c) -> p c e", c=4)
                    of = [[src_f[:, :], dst_f[:, :], raw_w[:, :] if L.n == 0 else y[:, 0, :]],
                          [y[:, 1, :], y[:, 2, :], y[:, 3, :]]][r]
                    for i, rows_in in enumerate(of):
                        last = nc.tensor.transpose(b_turn[:, P * i:P * (i + 1)], rows_in, ident[:, :])
                last.then_inc(L.turned, 1)

            def hidden1(L, p, macro, r, chunk, n_before):
                pe.wait_ge(L.turned_out, L.rounds * (L.preps_before(p) + macro + 1) + 1)
                pe.wait_ge(L.mlp_out, n_before + 1)
                col = ITEMS * (chunk % (2 * CHUNKS))
                for e in range(4):
                    last = mm(b_mlp[:, P * e:P * (e + 1)], a1_blocks[:, 4 * r + e, :], ef_t[:, :, ds(col, ITEMS)],
                              start=True, stop=True)
                last.then_inc(L.mlp, 1)

            def hidden2(L, r, n_before):
                pe.wait_ge(L.mlp_out, n_before + 1)
                mm(b_mlp[:, :], a2_pair[:, :], hid1[:, 4 * r:4 * r + 4, :].rearrange("p q e -> p (q e)"),
                   start=True, stop=True).then_inc(L.mlp, 1)

            def edge_weights(L, p, j, item):
                pe.wait_ge(L.mixed, p * NIT + FREE + item - 1)
                mm(b_w[j % 2][:, 0:2 * P], hid2[:, j, :], a3_pair[:, :], start=True, stop=True).then_inc(L.weights, 1)

            for L in layers:
                if L.n == 1:
                    pe.wait_ge(up_out, NBG + 1)
                with pe.Fori(0, passes) as p:
                    pe.wait_ge(L.plan, p + 1)
                    for a in range(LAG):
                        mm(bank[4 + a][:, 0:2 * P], zeros[:, :], a1_blocks[:, 0:2, :].rearrange("p e h -> p (e h)"),
                           start=True, stop=True).then_inc(L.sums, 1)
                    for r in range(L.rounds):
                        turn(L, p, 0, r)
                    if L.n == 1:
                        done = p * (3 + 4 * NCH)
                        hidden1(L, p, 0, 0, 0, done)
                        hidden1(L, p, 0, 1, 0, done + 1)
                        hidden2(L, 0, done + 2)
                        pe.wait_ge(L.mlp_out, done + 4)
                        edge_weights(L, p, 0, 0)

                    def walk_chunk(m, c):
                        chunk = m * CHUNKS + c
                        done = p * (3 + 4 * NCH) + 3 + 4 * chunk
                        first = isinstance(c, int)
                        if L.n == 1:
                            hidden2(L, 1, done)
                        for j in range(ITEMS):
                            a = j % 2
                            item = chunk * ITEMS + j
                            if first and j in TURN_AT[:L.rounds]:
                                turn(L, p, m + 1, TURN_AT.index(j))
                            if L.n == 1:
                                if j == 3:
                                    pe.wait_ge(L.mlp_out, done + 2)
                                if j == ITEMS - 1:
                                    pe.wait_ge(L.mlp_out, done + 5)
                                edge_weights(L, p, (j + 1) % ITEMS, item + 1)
                            if L.n == 0 and j % 2 == 0:
                                pe.wait_ge(L.quad[j // 2], 64 * (p * NCH + chunk) + 64)
                            if L.n == 0:
                                pe.wait_ge(L.hot_ready, p * NIT + item + 1)
                            else:
                                pe.wait_ge(L.mixed, p * NIT + FREE + item + 1)
                            for half in range(L.n + 1):
                                for k in range(2):
                                    of = rows[:, 2 * j + k, :] if L.n == 0 else \
                                        msg[:, a, 2 * k + half, :, :].rearrange("p c u -> p (c u)")
                                    last = mm(bank[4 + a][:, P * half:P * (half + 1)], of, hot[:, a, k, :],
                                              start=k == 0, stop=k == 1)
                            last.then_inc(L.sums, 1)
                            if L.n == 1 and j in (0, 2):
                                hidden1(L, p, m if first else m + 1, j // 2, chunk + 1, done + 1 + j // 2)
                            if L.n == 1 and j == 4:
                                hidden2(L, 0, done + 3)

                    with pe.Fori(0, MACROS) as m:
                        walk_chunk(m, 0)
                        with pe.Fori(1, CHUNKS) as c:
                            walk_chunk(m, c)

                if L.n == 0:
                    pe.sem_inc(lin_ready, NH)
                    pe.sem_inc(h_turned, 1)
                    pe.sem_inc(up_ready, 1)

                    def linear(t):
                        pe.wait_ge(x1_ready, t + 1)
                        for h in range(NH):
                            pe.wait_ge(sums_in, NH * t + h + 1)
                            for g in blocks_in(h):
                                h, at = where(g)
                                last = mm(bank[h][:, at:at + P], sums_st[:, g * P:(g + 1) * P], w_t[:, :],
                                          start=True, stop=True)
                            last.then_inc(lin_ready, 1)

                    def table_rows(t):
                        pe.wait_ge(h_copied, t + 1)
                        pe.wait_ge(normed, NBG + t + 2)
                        for g in range(GB):
                            h, at = where(g)
                            last = nc.tensor.transpose(bank[2 + h][:, at:at + P], h_st[:, g * P:(g + 1) * P], ident[:, :])
                        last.then_inc(h_turned, 1)
                        pe.wait_ge(up_out, t + 1)
                        pe.wait_ge(h_copied, t + 2)
                        for g in range(GB):
                            h, at = where(g)
                            last = mm(bank[4 + h][:, at:at + P], h_turn[:, g * P:(g + 1) * P], w_up[:, :],
                                      start=True, stop=True)
                        last.then_inc(up_ready, 1)

                    linear(0)
                    with pe.Fori(0, NBG - 1) as t:
                        linear(t + 1)
                        table_rows(t)
                    table_rows(NBG - 1)

            pe.sem_inc(fin_ready, NH)
            with pe.Fori(0, NBG) as t:
                for h in range(NH):
                    pe.wait_ge(fin_out, NH * t + h + 1)
                    pe.wait_ge(fin_staged, NH * t + h + 1)
                    for g in blocks_in(h):
                        at = where(g)[1]
                        for k in range(2):
                            last = mm(bank[h][:, at:at + P], fin_sums[:, (2 * g + k) * P:(2 * g + k + 1) * P], w_out[:, k, :],
                                      start=k == 0, stop=k == 1)
                    last.then_inc(fin_ready, 1)


_INS = ['x', 'src', 'dst', 'edge_attr_4', 'edge_attr_8', 'edge_weight', 'L0_gnn_W', 'L0_gnn_b', 'L1_gnn_W_up_s',
        'L1_gnn_W_up_v', 'L1_gnn_A1', 'L1_gnn_b1', 'L1_gnn_A2', 'L1_gnn_b2', 'L1_gnn_A3', 'L1_gnn_W_out_s',
        'L1_gnn_W_out_v']


def kernel(**inputs):
    import numpy as _np
    import concourse.bacc as _bacc
    from concourse import mybir as _mybir
    from concourse.bass_utils import run_bass_kernel_spmd as _run

    nc = _bacc.Bacc("TRN2", target_bir_lowering=False, num_devices=1)
    arrays, args = {}, []
    for name in _INS:
        a = _np.ascontiguousarray(inputs[name])
        arrays[f"in_{name}_dram"] = a
        args.append(nc.dram_tensor(f"in_{name}_dram", a.shape, _mybir.dt.from_np(a.dtype), kind="ExternalInput").ap())
    shape = inputs['x'].shape
    args.append(nc.dram_tensor("out_0_dram", shape, _mybir.dt.float32, kind="ExternalOutput").ap())
    build_gnn(nc, *args)
    r = _run(nc, [arrays], core_ids=[0])
    return r.results[0]["out_0_dram"]
```

```python
import math

import concourse.bass as bass
from concourse import mybir
from contextlib import ExitStack

P = 128
SLOTS = 16
ITEMS = SLOTS // 2
QUADS = SLOTS // 4
CHUNKS = 8
MACRO_ITEMS = CHUNKS * ITEMS
assert MACRO_ITEMS * 2 == P
MUL = 32
NE8 = 8


def divisor(n, most):
    return max(d for d in range(1, most + 1) if n % d == 0)


def build_gnn(nc, x, src, dst, ea4, ea8, ew, W, b, Wus, Wuv, A1, b1, A2, b2, A3, Wos, Wov, out):
    f32, i32 = mybir.dt.float32, mybir.dt.int32
    ALU, ACT, AX = mybir.AluOpType, mybir.ActivationFunctionType, mybir.AxisListType
    ds = bass.ds

    N, E = x.shape[0], src.shape[0]
    NB = -(-N // P)
    TAIL = N - (NB - 1) * P
    TILES = E // P
    assert E % P == 0 and x.shape[1] == P
    PAIRS = -(-TILES // 2)
    FULL = E // (2 * P)
    MACROS = -(-(PAIRS + NB - 1) // MACRO_ITEMS)
    COLS = MACROS + 1
    NCH = MACROS * CHUNKS
    NIT = MACROS * MACRO_ITEMS
    GB = divisor(NB, min(8, NB // 4))
    NBG = NB // GB
    GW = GB * P
    EPS = 1e-5
    INV_UP = 1.0 / math.sqrt(MUL)
    INV_OUT = 1.0 / math.sqrt(2 * MUL) / 10.0
    INV_R3 = 1.0 / math.sqrt(3.0)
    NOWHERE = 1.0e6
    R1 = divisor(E, P)
    C1 = E // R1
    R2 = divisor(FULL, P)
    C2 = FULL // R2
    ROW = NIT + 8
    WINDOW = min(MACRO_ITEMS, FULL)
    ROWS = WINDOW + 1
    assert 2 * COLS <= P
    TURN_AT, COPY_AT = [0, 1, 3, 5], [2, 3, 5, 7]
    PLACES = 2
    TERMS = 32
    LAG = 2
    FREE = ITEMS

    pairs_of = lambda ap: (ap[0:FULL * 2 * P].rearrange("(t e) -> t e", e=2 * P) if len(ap.shape) == 1 else
                           ap[0:FULL * 2 * P].rearrange("(t e) c -> t (e c)", e=2 * P))
    last_of = lambda ap: (ap[E - P:E].rearrange("(a t e) -> a t e", a=1, t=1) if len(ap.shape) == 1 else
                          ap[E - P:E].rearrange("(a t e) c -> a t (e c)", a=1, t=1))

    h0_table = nc.dram_tensor("h0_table", (NB * P, P), f32, kind="Internal").ap()
    up_table = nc.dram_tensor("up_table", (NB * P, P), f32, kind="Internal").ap()
    x1_table = nc.dram_tensor("x1_table", (NB * P, P), f32, kind="Internal").ap()
    plan_dram = nc.dram_tensor("plan_dram", (2 * COLS, MACRO_ITEMS), f32, kind="Internal").ap()

    with ExitStack() as ctx:
        def sb(name, shape, dt=f32):
            return ctx.enter_context(nc.sbuf_tensor(name, shape, dt))

        def sem(name):
            return ctx.enter_context(nc.semaphore(name))

        zeros = sb("zeros", [P, P])
        arena = sb("arena", [P, max(NB * P, 72 * P + PLACES * TERMS * MUL)])
        agg = sb("agg", [P, NB * 2 * P])
        ident = sb("ident", [P, P])
        ones = sb("ones", [P, P])
        iota_free = sb("iota_free", [P, P])
        w_t = sb("w_t", [P, P])
        bias_all = sb("bias_all", [P, P])
        w_up = sb("w_up", [P, P])
        a1_blocks = sb("a1_blocks", [P, NE8, P])
        a2_pair = sb("a2_pair", [P, P])
        a3_pair = sb("a3_pair", [P, 2 * P])
        b1_col = sb("b1_col", [P, 1])
        b2_col = sb("b2_col", [P, 1])
        w_out = sb("w_out", [P, 2, P])
        item_of = sb("item_of", [P, COLS])
        block_of = sb("block_of", [P, COLS])
        pair_of = sb("pair_of", [P, COLS])
        late = sb("late", [P, COLS])
        first_pair = sb("first_pair", [1, COLS])
        first_pair_i = sb("first_pair_i", [1, COLS], i32)
        row_of = sb("row_of", [P, COLS])
        row_of_all = sb("row_of_all", [ROWS, COLS * MACRO_ITEMS])
        shift = sb("shift", [P, COLS])
        small = sb("small", [P, 8])
        small_i = sb("small_i", [P, 4], i32)
        flag = sb("flag", [P, 4])
        row_f = sb("row_f", [1, ROW])
        row_i = sb("row_i", [1, ROW], i32)
        stats = sb("stats", [P, GB, 6])
        moments = sb("moments", [P, GB, 2])
        spread = sb("spread", [P, GB])
        deviations = sb("deviations", [P, GB])
        scales = sb("scales", [P, 2, GB])
        raw_ends = sb("raw_ends", [P, 2, 2 * P], i32)
        ends_f = sb("ends_f", [P, 2, 2 * P])
        raw_w = sb("raw_w", [P, 2 * P])
        chosen = sb("chosen", [P, MACRO_ITEMS])
        moved = sb("moved", [P, P])
        src_t = sb("src_t", [P, 2, P])
        dst_t = sb("dst_t", [P, 2, P])
        w_edge = sb("w_edge", [P, 2, P])
        picks = sb("picks", [P, SLOTS], i32)
        rows = sb("rows", [P, SLOTS, P])
        hot = sb("hot", [P, 2, 2, P])

        place = [0]

        def part(width):
            place[0] += width
            assert place[0] <= arena.shape[1]
            return arena[:, place[0] - width:place[0]]

        raw_ea = part(4 * 2 * P)
        raw_ef = part(2 * NE8 * P).rearrange("p (b k w) -> p b k w", b=16, k=2)[0:ROWS]
        ef_t = part(16 * P).rearrange("p (b q) -> p b q", b=16)
        y_edge = part(4 * 2 * P).rearrange("p (c k q) -> p c k q", c=4, k=2)
        hid1 = part(ITEMS * P).rearrange("p (q e) -> p q e", q=ITEMS)
        hid2 = part(ITEMS * P).rearrange("p (q e) -> p q e", q=ITEMS)
        scaled = part(PLACES * TERMS * MUL).rearrange("p (a c u) -> p a c u", a=PLACES, c=TERMS)
        msg = part(2 * 4 * P).rearrange("p (a r c u) -> p a r c u", a=2, r=4, c=4)

        fin = arena[:, 24 * P:24 * P + 4 * GW]
        assert 4 * GW <= 32 * P
        fin_sums = rows[:, :, :].rearrange("p s d -> p (s d)")[:, 0:2 * GW]
        raw_w_out = rows[:, 0, :]
        spare = lambda i: agg[:, NB * P + i * GW:NB * P + (i + 1) * GW]
        sums_st, h_st, h_turn, up_st = (spare(i) for i in range(4))
        started = agg[:, NB * P:NB * P + COLS * (NB - 1)].rearrange("p (c b) -> p c b", c=COLS)
        HALVES = [(0, min(GW, 512)), (min(GW, 512), GW)]
        HALVES = [h for h in HALVES if h[1] > h[0]]
        NH = len(HALVES)
        blocks_in = lambda h: range(HALVES[h][0] // P, HALVES[h][1] // P)
        where = lambda g: (g * P // 512, g * P % 512)

        bank = [ctx.enter_context(nc.psum_tensor(f"bank{i}", [P, 512], f32)) for i in range(8)]
        b_w = [bank[0], bank[2]]
        b_iota = bank[1][:, 0:P]
        b_y2 = bank[1][:, P:2 * P].rearrange("p (k q) -> p k q", k=2)
        b_mlp, b_turns = bank[6], [bank[7], bank[3]]

        x_zeroed = sem("x_zeroed")
        x_in = sem("x_in")
        order_in = sem("order_in")
        w_zeroed = sem("w_zeroed")
        w_in = sem("w_in")
        w_set = sem("w_set")
        consts = sem("consts")
        votes = sem("votes")
        counted = sem("counted")
        chain = sem("chain")
        passes_ready = sem("passes_ready")
        plan_out = sem("plan_out"); plan_stored = sem("plan_stored"); plan_in = sem("plan_in")
        pool_turn = sem("pool_turn"); act_turn = sem("act_turn"); dve_turn = sem("dve_turn")
        pe_turn = sem("pe_turn"); sp_turn = sem("sp_turn")
        stats_done = sem("stats_done"); var_ready = sem("var_ready"); sd_ready = sem("sd_ready")
        ln_ready = sem("ln_ready")
        agg_zeroed = sem("agg_zeroed")
        biased = sem("biased")
        normed = sem("normed")
        h_stored = sem("h_stored"); h_saved = sem("h_saved")
        table_ready = sem("table_ready")
        sums_in = sem("sums_in")
        lin_ready = sem("lin_ready"); x1_ready = sem("x1_ready"); x1_stored = sem("x1_stored")
        h_turned = sem("h_turned"); h_copied = sem("h_copied")
        up_ready = sem("up_ready"); up_out = sem("up_out"); up_stored = sem("up_stored"); up_saved = sem("up_saved")
        fin_staged = sem("fin_staged"); fin_x = sem("fin_x"); fin_ready = sem("fin_ready")
        fin_out = sem("fin_out"); fin_stored = sem("fin_stored"); fin_saved = sem("fin_saved")

        class Layer:
            def __init__(self, n):
                s = lambda name: sem(f"{name}_{n}")
                self.n = n
                self.rounds = (1, 4)[n]
                self.loads = (3, 5)[n]
                self.table = (h0_table, up_table)[n]
                self.plan = s("plan")
                self.plan_step = s("plan_step")
                self.meta_in = s("meta_in")
                self.floats = s("floats")
                self.turned = s("turned")
                self.turned_out = s("turned_out")
                self.picks_ready = s("picks_ready")
                self.quad = [s(f"quad{q}") for q in range(QUADS)]
                self.sums = s("sums")
                self.added = s("added")
                self.walked = s("walked")
                if n == 0:
                    self.hot_ready = s("hot_ready")
                else:
                    self.mlp = s("mlp")
                    self.mlp_out = s("mlp_out")
                    self.weights = s("weights")
                    self.scaled = s("scaled")
                    self.y_set = s("y_set")
                    self.third = s("third")
                    self.dots = s("dots")
                    self.mixed = s("mixed")
                self.used = self.sums if n == 0 else self.mixed

            def used_before(self, p):
                return p * (NIT + LAG) + LAG + FREE if self.n == 0 else p * NIT + FREE

            def sums_before(self, p):
                return p * (NIT + LAG) + (FREE if self.n == 0 else 0)

            def loaded(self, p, macro):
                return 16 * (self.loads * (self.preps_before(p) + macro + 1) + 3)

            def preps_before(self, p):
                return p * (MACROS + 1)

        layers = [Layer(0), Layer(1)]

        def after(eng, turn, semaphore, value):
            eng.wait_ge(semaphore, value)
            eng.sem_inc(turn, 1)

        loads = [(bias_all[:, :], b.rearrange("(a n) -> a n", a=1).to_broadcast([P, P])), (w_up[0:MUL, 0:MUL], Wus)]
        for i in range(3):
            loads.append((w_up[MUL + i:MUL + i + 3 * MUL - 2:3, MUL * (i + 1):MUL * (i + 2)], Wuv))
        for k in range(2):
            lo = 64 * k
            for e in range(NE8):
                loads.append((a1_blocks[lo + 8 * e:lo + 8 * e + 8, e, lo:lo + 64], A1))
            loads.append((a2_pair[lo:lo + 64, lo:lo + 64], A2))
            for at, w in ((2 * k, 2), (2 * k + 1, 1), (2 * k + 4, 0), (2 * k + 5, 3)):
                loads.append((a3_pair[lo:lo + 64, MUL * at:MUL * (at + 1)], A3[:, MUL * w:MUL * (w + 1)]))
            loads.append((b1_col[lo:lo + 64, :], b1.rearrange("(n a) -> n a", a=1)))
            loads.append((b2_col[lo:lo + 64, :], b2.rearrange("(n a) -> n a", a=1)))
            loads.append((raw_w_out[0:MUL, MUL * k:MUL * (k + 1)], Wos[MUL * k:MUL * (k + 1), :]))
            for i in range(3):
                loads.append((raw_w_out[MUL * (i + 1):MUL * (i + 2), MUL * k:MUL * (k + 1)],
                              Wov[MUL * (1 - k):MUL * (2 - k), :]))

        block = ctx.enter_context(nc.Block())

        @block.sync
        def _(sp):
            rows_of = lambda table, t: table[ds(t * GW, GW), :].rearrange("(b p) d -> p b d", p=P)
            cut = lambda ap: ap.rearrange("p (b d) -> p b d", d=P)
            sp.dma_start(agg[0:R1, 0:C1].bitcast(i32), dst.rearrange("(r c) -> r c", r=R1)).then_inc(order_in, 16)
            sp.dma_start(agg[0:R2, C1:C1 + 2 * P * C2].bitcast(i32),
                         dst[0:FULL * 2 * P].rearrange("(r c) -> r c", r=R2)).then_inc(order_in, 16)
            sp.dma_start(small_i[0:R1 - 1, 0:1], dst.rearrange("(r c) -> r c", r=R1)[1:R1, 0:1],
                         allow_slow_non_contiguous=True).then_inc(order_in, 16)
            sp.dma_start(w_t[:, :], W).then_inc(order_in, 16)
            sp.wait_ge(x_zeroed, 1)
            sp.dma_start(cut(arena[:, 0:(NB - 1) * P]),
                         x[0:(NB - 1) * P, :].rearrange("(b p) d -> p b d", p=P)).then_inc(x_in, 16)
            sp.dma_start(arena[0:TAIL, (NB - 1) * P:NB * P], x[(NB - 1) * P:N, :]).then_inc(x_in, 16)
            sp.wait_ge(w_zeroed, 1)
            for to, of in loads:
                sp.dma_start(to, of).then_inc(w_in, 16)
            sp.wait_ge(plan_out, 1)
            sp.wait_ge(passes_ready, 1)
            sp.dma_start(plan_dram, agg[0:2 * COLS, 0:MACRO_ITEMS]).then_inc(plan_stored, 16)
            sp.wait_ge(plan_stored, 16)
            sp.dma_start(row_f[0:1, LAG:NIT + LAG],
                         plan_dram[0:MACROS, :].rearrange("(a m) q -> a (m q)", a=1)).then_inc(plan_in, 16)
            sp.dma_start(row_of_all[:, :], plan_dram[COLS:2 * COLS, :].rearrange("(a m) q -> a (m q)", a=1)
                         .to_broadcast([ROWS, COLS * MACRO_ITEMS])).then_inc(plan_in, 16)
            passes = sp.value_load(small_i[0:1, 2:3], min_val=1, max_val=NB)

            edge_data = [[(raw_ends[:, 0, :], src), (raw_ends[:, 1, :], dst), (raw_w[:, :], ew)],
                         [(raw_ends[:, 0, :], src), (raw_ends[:, 1, :], dst), (raw_ea, ea4)]]

            def load_last(L):
                for to, of in edge_data[L.n][2 * L.n:]:
                    sp.dma_start(to[WINDOW:ROWS, :].rearrange("p (k w) -> p k w", k=2),
                                 last_of(of).to_broadcast([1, 2, to.shape[1] // 2])).then_inc(L.meta_in, 16)
                if L.n == 1:
                    for k in range(2):
                        sp.dma_start(raw_ef[WINDOW:ROWS, :, k, :], last_of(ea8)[:, 0, :].rearrange("t (b w) -> t b w", b=16)
                                     ).then_inc(L.meta_in, 16)

            def load_edges(L, p, macro):
                after(sp, sp_turn, L.turned, L.rounds * (L.preps_before(p) + macro) + 1)
                first = sp.value_load(first_pair_i[0:1, ds(macro, 1)], min_val=0, max_val=FULL - WINDOW)
                for to, of in edge_data[L.n]:
                    sp.dma_start(to[0:WINDOW, :], pairs_of(of)[ds(first, WINDOW), :]).then_inc(L.meta_in, 16)
                if L.n == 1:
                    for k in range(2):
                        half = pairs_of(ea8)[ds(first, WINDOW), NE8 * P * k:NE8 * P * (k + 1)]
                        sp.dma_start(raw_ef[0:WINDOW, :, k, :], half.rearrange("t (b w) -> t b w", b=16)
                                     ).then_inc(L.meta_in, 16)

            def load_all_edges(L):
                with sp.Fori(0, passes) as p:
                    with sp.Fori(1, MACROS + 1) as macro:
                        load_edges(L, p, macro)
                    load_edges(L, p + 1, 0)
                after(sp, sp_turn, L.meta_in, L.loaded(passes, 0))

            sp.sem_inc(layers[0].turned, 1)
            load_last(layers[0])
            load_edges(layers[0], 0, 0)
            sp.sem_inc(h_saved, 2)
            with sp.Fori(0, NBG) as t:
                sp.wait_ge(normed, t + 2)
                sp.dma_start(rows_of(h0_table, t), cut(agg[:, ds(NB * P + (t % 2) * GW, GW)])).then_inc(h_stored, 16)
                after(sp, h_saved, h_stored, 16 * t + 16)
            sp.sem_inc(table_ready, 1)
            load_all_edges(layers[0])
            sp.sem_inc(up_saved, 1)
            with sp.Fori(0, NBG) as t:
                sp.wait_ge(x1_ready, t + 2)
                sp.dma_start(rows_of(x1_table, t), cut(arena[:, ds(t * GW, GW)])).then_inc(x1_stored, 16)
                sp.wait_ge(up_out, t + 2)
                sp.dma_start(rows_of(up_table, t), cut(up_st)).then_inc(up_stored, 16)
                after(sp, up_saved, up_stored, 16 * t + 16)
            sp.wait_ge(x1_stored, 16 * NBG)
            sp.sem_inc(table_ready, 1)
            sp.sem_inc(layers[1].turned, 1)
            load_last(layers[1])
            load_edges(layers[1], 0, 0)
            load_all_edges(layers[1])
            sp.wait_ge(layers[1].walked, 1)
            fin_x1 = lambda t: fin[:, ds((t % 2) * GW, GW)]
            fin_st = lambda t: fin[:, ds(2 * GW + (t % 2) * GW, GW)]

            sp.dma_start(cut(fin_x1(0)), rows_of(x1_table, 0)).then_inc(fin_x, 16)
            with sp.Fori(0, NBG - 1) as t:
                after(sp, sp_turn, fin_x, 16 * t + 16)
                after(sp, sp_turn, fin_out, NH * t + NH)
                sp.dma_start(cut(fin_x1(t + 1)), rows_of(x1_table, t + 1)).then_inc(fin_x, 16)
                sp.wait_ge(fin_out, NH * t + 2 * NH)
                sp.dma_start(rows_of(out, t), cut(fin_st(t))).then_inc(fin_stored, 16)
                after(sp, fin_saved, fin_stored, 16 * t + 16)
            sp.wait_ge(fin_out, NH * NBG + NH)
            st = fin[:, 2 * GW + (NBG - 1) % 2 * GW:][:, 0:GW]
            last = (NBG - 1) * GW
            if GB > 1:
                sp.dma_start(out[last:last + GW - P, :].rearrange("(b p) d -> p b d", p=P),
                             cut(st[:, 0:GW - P])).then_inc(fin_stored, 16)
            sp.dma_start(out[last + GW - P:N, :], st[0:TAIL, GW - P:GW]).then_inc(fin_stored, 16)
            sp.wait_ge(fin_stored, 16 * (NBG - 1 + (2 if GB > 1 else 1)))

        @block.gpsimd
        def _(pool):
            nc.gpsimd.memset(ones[:, :], 1.0).then_inc(consts, 1)
            exact = dict(allow_small_or_imprecise_dtypes=True)
            nc.gpsimd.iota(iota_free[:, :], [[1, P]], base=0, channel_multiplier=0, **exact).then_inc(consts, 1)
            nc.gpsimd.iota(item_of[:, :], [[MACRO_ITEMS, COLS]], base=0, channel_multiplier=0, **exact).then_inc(consts, 1)
            nc.gpsimd.iota(small_i[:, 1:2], [[1, 1]], base=0, channel_multiplier=1).then_inc(consts, 1)
            nc.gpsimd.iota(hot[:, 0, 0, 0:NB - 1], [[P, NB - 1]], base=P, channel_multiplier=0, **exact).then_inc(consts, 1)
            pool.wait_ge(consts, 5)
            nc.gpsimd.affine_select(out=ident[:, :], in_=ones[:, :], compare_op=ALU.is_equal, fill=0.0,
                                    base=0, pattern=[[-1, P]], channel_multiplier=1).then_inc(consts, 1)
            pool.wait_ge(passes_ready, 1)
            passes = pool.value_load(small_i[0:1, 2:3], min_val=1, max_val=NB)

            pool.wait_ge(layers[0].plan, 1)
            nc.gpsimd.memset(agg[:, 0:NB * P], 0.0).then_inc(agg_zeroed, 1)
            pool.wait_ge(w_in, 16 * len(loads))
            with pool.Fori(0, NBG) as t:
                after(pool, pool_turn, normed, t + 2)
                x_step = arena[:, ds(t * GW, GW)].rearrange("p (b d) -> p b d", d=P)
                nc.gpsimd.tensor_tensor(x_step, x_step, bias_all[:, :].unsqueeze(1).to_broadcast([P, GB, P]),
                                        ALU.add).then_inc(biased, 1)

            for L in layers:
                pool.sem_inc(L.used, FREE)
                if L.n == 1:
                    pool.wait_ge(layers[0].walked, 1)
                    nc.gpsimd.memset(agg[:, NB * P + 4 * GW:2 * NB * P], 0.0).then_inc(agg_zeroed, 1)
                    with pool.Fori(0, NBG) as t:
                        after(pool, pool_turn, lin_ready, NH * t + 2 * NH)
                        nc.gpsimd.tensor_copy(agg[:, ds(t * GW, GW)].rearrange("p (b n) -> p b n", n=P),
                                              zeros[:, :].unsqueeze(1).to_broadcast([P, GB, P])).then_inc(agg_zeroed, 1)
                    pool.wait_ge(table_ready, 2)
                with pool.Fori(0, passes) as p:
                    after(pool, pool_turn, L.plan, p + 1)
                    after(pool, pool_turn, table_ready, L.n + 1)
                    after(pool, pool_turn, w_set, 1)
                    with pool.Fori(0, MACROS) as m:
                        with pool.Fori(0, CHUNKS) as c:
                            chunk = m * CHUNKS + c
                            for q in range(QUADS):
                                after(pool, pool_turn, L.picks_ready, QUADS * (p * (NCH + 1) + chunk) + q + 1)
                                after(pool, pool_turn, L.used,
                                      L.used_before(p) + ITEMS * chunk + 2 * q + 2 - ITEMS)
                                for s in range(4 * q, 4 * q + 4):
                                    pool.indirect_dma_start(
                                        out=rows[:, s, :], out_offset=None, in_=L.table[:, :],
                                        in_offset=bass.IndirectOffsetOnAxis(ap=picks[:, s:s + 1], axis=0),
                                    ).then_inc(L.quad[q], 16)

        @block.scalar
        def _(act):
            def copy(to, of, **k):
                return nc.scalar.activation(to, of, ACT.Copy, **k)

            def deviation(count):
                act.wait_ge(var_ready, count + 1)
                nc.scalar.activation(deviations[:, :], spread[:, :], ACT.Sqrt).then_inc(sd_ready, 1)

            def norm(t, count, to):
                after(act, act_turn, ln_ready, count + 1)
                for g in range(GB):
                    last = nc.scalar.activation(to(g), arena[:, ds(t * GW + g * P, P)], ACT.Relu,
                                                bias=scales[:, 1, g:g + 1], scale=scales[:, 0, g:g + 1])
                last.then_inc(normed, 1)

            with act.Fori(0, NBG) as t:
                deviation(t)
                after(act, act_turn, h_saved, t + 1)
                norm(t, t, lambda g: agg[:, ds(NB * P + (t % 2) * GW + g * P, P)])

            act.wait_ge(passes_ready, 1)
            passes = act.value_load(small_i[0:1, 2:3], min_val=1, max_val=NB)

            def copy_turned(L, p, macro, r):
                at = (macro % 2) * MACRO_ITEMS
                b_turn = b_turns[r % 2]
                after(act, act_turn, L.turned, L.rounds * (L.preps_before(p) + macro) + r + 2)
                if r >= 2:
                    last = copy(ef_t[:, 8 * (r - 2):8 * (r - 1), ds(at, MACRO_ITEMS)],
                                b_turn[:, :].rearrange("p (b q) -> p b q", b=8))
                else:
                    tables = [[src_t[:, :, :], dst_t[:, :, :], w_edge[:, :, :] if L.n == 0 else y_edge[:, 0]],
                              [y_edge[:, 1], y_edge[:, 2], y_edge[:, 3]]][r]
                    for i, table in enumerate(tables):
                        last = copy(table[:, :, ds(at, MACRO_ITEMS)],
                                    b_turn[:, P * i:P * (i + 1)].rearrange("p (k q) -> p k q", k=2))
                last.then_inc(L.turned_out, 1)

            def tables_stand(L, p, macro):
                after(act, act_turn, L.turned_out, L.rounds * (L.preps_before(p) + macro + 1) + 1)

            def copy_picks(L, q, chunk):
                first = ITEMS * (chunk % (2 * CHUNKS)) + 2 * q
                copy(picks[:, 4 * q:4 * q + 4].rearrange("p (j k) -> p k j", k=2),
                     src_t[:, :, ds(first, 2)]).then_inc(L.picks_ready, 1)

            def scale_rows(L, p, j, item, col):
                act.wait_ge(L.mixed, p * NIT + FREE + item + 1 - PLACES)
                act.sem_inc(act_turn, 1)
                for k in range(2):
                    row = rows[:, 2 * j + k, :].rearrange("p (c u) -> p c u", u=MUL)
                    to = scaled[:, j % PLACES]
                    part_i = to.rearrange("p (c k m) u -> p k c m u", c=2, k=2)[:, k]
                    y = lambda c: y_edge[:, c, k, ds(col, 1)]
                    copy(to[:, 8 * k:8 * k + 4, :], row, scale=y(0))
                    for i in range(2):
                        last = copy(part_i[:, :, 5 + i, :], row[:, 0:2 + i:1 + i, :], scale=y(1 + i))
                last.then_inc(L.scaled, 1)

            def silu_hidden1(L, r, n_before):
                act.wait_ge(L.mlp, n_before + 1)
                nc.scalar.activation(
                    hid1.rearrange("p q (b e) -> p e b q", e=NE8)[:, 4 * r:4 * r + 4],
                    b_mlp[:, :].rearrange("p (e b q) -> p e b q", e=4, b=16), ACT.Silu,
                    bias=b1_col[:, 0:1]).then_inc(L.mlp_out, 1)

            def silu_hidden2(L, r, n_before):
                act.wait_ge(L.mlp, n_before + 1)
                nc.scalar.activation(
                    hid2[:, 4 * r:4 * r + 4, :], b_mlp[:, :].rearrange("p (q e) -> p q e", q=4), ACT.Silu,
                    bias=b2_col[:, 0:1]).then_inc(L.mlp_out, 1)

            act.wait_ge(w_set, 1)
            for L in layers:
                act.sem_inc(L.turned_out, 1)
                if L.n == 1:
                    act.sem_inc(L.mlp_out, 1)
                with act.Fori(0, passes) as p:
                    after(act, act_turn, L.used, L.used_before(p))
                    copy_turned(L, p, 0, 0)
                    after(act, act_turn, L.turned_out, L.rounds * L.preps_before(p) + 2)
                    for q in range(QUADS):
                        copy_picks(L, q, 0)
                    if L.n == 1:
                        for r in range(1, L.rounds):
                            copy_turned(L, p, 0, r)
                        tables_stand(L, p, 0)
                        done = p * (3 + 4 * NCH)
                        silu_hidden1(L, 0, done)
                        silu_hidden1(L, 1, done + 1)
                        silu_hidden2(L, 0, done + 2)

                    def walk_chunk(m, c):
                        chunk = m * CHUNKS + c
                        done = p * (3 + 4 * NCH) + 3 + 4 * chunk
                        first = isinstance(c, int)
                        for q in range(QUADS):
                            after(act, act_turn, L.quad[q], 64 * (p * NCH + chunk) + 64)
                            copy_picks(L, q, chunk + 1)
                            if L.n == 0:
                                continue
                            for j in (2 * q, 2 * q + 1):
                                scale_rows(L, p, j, chunk * ITEMS + j, ITEMS * (chunk % (2 * CHUNKS)) + j)
                                if first and j in COPY_AT:
                                    copy_turned(L, p, m + 1, COPY_AT.index(j))
                            if q == 0:
                                silu_hidden2(L, 1, done)
                            elif q < 3:
                                silu_hidden1(L, q - 1, done + q)
                            else:
                                silu_hidden2(L, 0, done + 3)

                    with act.Fori(0, MACROS) as m:
                        if L.n == 0:
                            after(act, act_turn, L.used, L.used_before(p) + m * MACRO_ITEMS)
                            copy_turned(L, p, m + 1, 0)
                        walk_chunk(m, 0)
                        tables_stand(L, p, m + 1)
                        with act.Fori(1, CHUNKS) as c:
                            walk_chunk(m, c)
                    after(act, act_turn, L.picks_ready, QUADS * (NCH + 1) * (p + 1))

                if L.n == 0:
                    act.sem_inc(up_out, 1)
                    act.wait_ge(L.walked, 1)

                    def stage_sums(t):
                        for h, (a, z) in enumerate(HALVES):
                            after(act, act_turn, lin_ready, NH * t + h + 1)
                            copy(sums_st[:, a:z], agg[:, ds(t * GW + a, z - a)]).then_inc(sums_in, 1)

                    def norm_step(t):
                        after(act, act_turn, h_turned, t + 1)
                        norm(t, NBG + t, lambda g: h_st[:, g * P:(g + 1) * P])

                    def table_step(t):
                        act.wait_ge(up_saved, t + 1)
                        after(act, act_turn, up_ready, t + 2)
                        for h, (a, z) in enumerate(HALVES):
                            last = copy(up_st[:, a:z], bank[4 + h][:, 0:z - a], scale=INV_UP)
                        last.then_inc(up_out, 1)

                    stage_sums(0)
                    stage_sums(1)
                    deviation(NBG)
                    norm_step(0)
                    stage_sums(2)
                    deviation(NBG + 1)
                    with act.Fori(1, NBG - 2) as t:
                        norm_step(t)
                        table_step(t - 1)
                        stage_sums(t + 2)
                        deviation(NBG + t + 1)
                    norm_step(NBG - 2)
                    table_step(NBG - 3)
                    deviation(2 * NBG - 1)
                    norm_step(NBG - 1)
                    table_step(NBG - 2)
                    table_step(NBG - 1)

            act.wait_ge(layers[1].walked, 1)
            with act.Fori(0, NBG) as t:
                for h, (a, z) in enumerate(HALVES):
                    after(act, act_turn, fin_ready, NH * t + h + 1)
                    copy(fin_sums[:, 2 * a:2 * z], agg[:, ds(t * 2 * GW + 2 * a, 2 * (z - a))]).then_inc(fin_staged, 1)

        @block.vector
        def _(dve):
            v = nc.vector
            links = [0]

            def link(ins):
                links[0] += 1
                ins.then_inc(chain, 1)
                dve.wait_ge(chain, links[0])

            v.memset(arena[:, (NB - 1) * P:NB * P], 0.0).then_inc(x_zeroed, 1)
            v.memset(w_up[:, :], 0.0)
            v.memset(a1_blocks[:, :, :], 0.0)
            v.memset(a3_pair[:, :], 0.0)
            v.memset(a2_pair[:, :], 0.0).then_inc(w_zeroed, 1)
            v.memset(zeros[:, :], 0.0)
            v.memset(w_out[:, :, :], 0.0)
            v.memset(row_f[:, :], 0.0)
            link(v.memset(small[:, :], 0.0))
            dve.wait_ge(consts, 6)

            dve.wait_ge(order_in, 64)
            d1 = agg[0:R1, 0:C1].bitcast(i32)
            falls = agg[0:R1, C1 + 2 * P * C2:2 * C1 + 2 * P * C2 - 1]
            link(v.tensor_tensor(falls, d1[:, 0:C1 - 1], d1[:, 1:C1], ALU.is_gt))
            link(v.tensor_reduce(small[0:R1, 0:1], falls, axis=AX.X, op=ALU.max))
            link(v.tensor_tensor(small[0:R1 - 1, 1:2], d1[0:R1 - 1, C1 - 1:C1], small_i[0:R1 - 1, 0:1], ALU.is_gt))
            d2 = agg[0:R2, C1:C1 + 2 * P * C2].bitcast(i32).rearrange("r (c e) -> r c e", e=2 * P)
            first_node = hot[:, 0, 0, 0:NB - 1]
            ends = hot[:, 0, 1, 0:C2]
            before = [hot[:, 1, 0, 0:NB - 1], hot[:, 1, 1, 0:NB - 1]]
            link(v.tensor_copy(ends[0:R2], d2[:, :, 2 * P - 1]))
            link(v.memset(before[1], 0.0))
            for c in range(C2):
                link(v.scalar_tensor_tensor(out=before[c % 2][0:R2], in0=first_node[0:R2], scalar=ends[0:R2, c:c + 1],
                                            in1=before[(c + 1) % 2][0:R2], op0=ALU.is_gt, op1=ALU.add))
            dve.sem_inc(votes, 1)
            dve.wait_ge(counted, 3)
            link(v.tensor_reduce(flag[:, 1:2], bank[0][:, 0:2], axis=AX.X, op=ALU.add))
            link(v.tensor_scalar(flag[:, 0:1], flag[:, 1:2], 1.0, None, ALU.min))
            link(v.tensor_scalar(flag[:, 1:2], flag[:, 0:1], -1.0, 1.0, ALU.mult, ALU.add))
            starts = before[C2 % 2]
            link(v.scalar_tensor_tensor(out=starts, in0=first_node, scalar=1.0 / P, in1=bank[1][:, 0:NB - 1],
                                        op0=ALU.mult, op1=ALU.add))
            link(v.tensor_scalar(small_i[:, 0:1], small_i[:, 1:2], MACRO_ITEMS - 1, None, ALU.bitwise_and))
            link(v.tensor_copy(small[:, 2:3], small_i[:, 0:1]))
            link(v.tensor_copy(small[:, 4:5], small_i[:, 1:2]))
            link(v.tensor_scalar(small[:, 3:4], small[:, 4:5], float(MACRO_ITEMS), None, ALU.is_ge))
            link(v.tensor_scalar(item_of[:, :], item_of[:, :], small[:, 2:3], None, ALU.add))
            for c in range(COLS):
                last = v.tensor_scalar(started[:, c, :], starts, item_of[:, c:c + 1], None, ALU.is_le)
            link(last)
            link(v.tensor_reduce(block_of[:, :], started, axis=AX.X, op=ALU.add))
            link(v.tensor_scalar(block_of[:, :], block_of[:, :], flag[:, 1:2], None, ALU.mult))
            link(v.tensor_tensor(pair_of[:, :], item_of[:, :], block_of[:, :], ALU.subtract))
            link(v.tensor_scalar(first_pair[:, :], pair_of[0:1, :], float(FULL - WINDOW), None, ALU.min))
            v.tensor_copy(first_pair_i[:, :], first_pair[:, :]).then_inc(votes, 1)
            dve.wait_ge(counted, 4)
            link(v.tensor_tensor(row_of[:, :], pair_of[:, :], bank[2][:, 0:COLS], ALU.subtract))
            link(v.tensor_scalar(row_of[:, :], row_of[:, :], float(WINDOW), None, ALU.min))
            link(v.memset(hot[:, 1, 0, :], 0.0))
            v.tensor_copy(hot[:, 1, 0, 0:COLS], block_of[:, :])
            v.tensor_copy(hot[:, 1, 0, COLS:2 * COLS], row_of[:, :]).then_inc(votes, 1)
            link(v.tensor_scalar(late[:, :], pair_of[:, :], 2.0, None, ALU.mult))
            link(v.tensor_scalar(late[:, :], late[:, :], small[:, 3:4], None, ALU.add))
            link(v.tensor_scalar(late[:, :], late[:, :], float(TILES - 1) + 0.5, NOWHERE, ALU.is_gt, ALU.mult))
            link(v.tensor_scalar(flag[:, 2:3], flag[:, 0:1], float(NB - 1), 1.0, ALU.mult, ALU.add))
            v.tensor_copy(small_i[:, 2:3], flag[:, 2:3]).then_inc(passes_ready, 1)
            dve.wait_ge(counted, 5)
            v.tensor_copy(agg[0:2 * COLS, 0:MACRO_ITEMS], bank[2][0:2 * COLS, 0:MACRO_ITEMS]).then_inc(plan_out, 1)
            v.tensor_copy(w_t[:, :], bank[3][:, 0:P])
            dve.wait_ge(plan_in, 32)
            dve.wait_ge(passes_ready, 1)
            passes = dve.value_load(small_i[0:1, 2:3], min_val=1, max_val=NB)

            def make_plan(L, p):
                if not isinstance(p, int):
                    dve.wait_ge(L.plan_step, 2 * p)
                v.tensor_scalar(row_i[:, :], row_f[:, :], flag[0:1, 3:4], None, ALU.add)
                v.tensor_scalar(shift[:, :], block_of[:, :], flag[:, 3:4], None, ALU.add).then_inc(L.plan_step, 1)
                dve.wait_ge(L.plan_step, 2 * p + 1)
                v.scalar_tensor_tensor(out=shift[:, :], in0=shift[:, :], scalar=-float(P), in1=late[:, :],
                                       op0=ALU.mult, op1=ALU.add).then_inc(L.plan, 1)
                dve.wait_ge(L.plan, p + 1)
                v.tensor_tensor(flag[:, 3:4], flag[:, 3:4], flag[:, 0:1], ALU.add).then_inc(L.plan_step, 1)

            link(v.memset(flag[:, 3:4], 0.0))
            make_plan(layers[0], 0)

            def row_stats(t, count):
                for g in range(GB):
                    last = v.bn_stats(stats[:, g, :], arena[:, ds(t * GW + g * P, P)])
                last.then_inc(stats_done, 1)
                after(dve, dve_turn, stats_done, 3 * count + 1)
                for g in range(GB):
                    last = v.bn_aggr(moments[:, g, :], stats[:, g, :])
                last.then_inc(stats_done, 1)
                dve.wait_ge(stats_done, 3 * count + 2)
                v.tensor_scalar(spread[:, :], moments[:, :, 1], EPS, None, ALU.add).then_inc(var_ready, 1)

            def row_scales(count):
                dve.wait_ge(normed, count + 1)
                dve.wait_ge(sd_ready, count + 1)
                v.reciprocal(scales[:, 0, :], deviations[:, :]).then_inc(stats_done, 1)
                dve.wait_ge(stats_done, 3 * count + 3)
                v.scalar_tensor_tensor(out=scales[:, 1, :], in0=moments[:, :, 0], scalar=-1.0, in1=scales[:, 0, :],
                                       op0=ALU.mult, op1=ALU.mult).then_inc(ln_ready, 1)

            dve.sem_inc(normed, 1)
            dve.wait_ge(x_in, 32)
            with dve.Fori(0, NBG) as t:
                row_stats(t, t)
                row_scales(t)

            dve.wait_ge(w_in, 16 * len(loads))
            v.tensor_copy(w_out[0:MUL, 0, 0:MUL], raw_w_out[0:MUL, 0:MUL])
            v.tensor_scalar(w_out[0:MUL, 1, 0:MUL], raw_w_out[0:MUL, MUL:2 * MUL], INV_R3, None, ALU.mult)
            for i in range(3):
                lo = MUL * (i + 1)
                last = v.tensor_copy(w_out[lo:lo + MUL, :, MUL + i:MUL + i + 3 * MUL - 2:3],
                                     raw_w_out[lo:lo + MUL, 0:2 * MUL].rearrange("p (k w) -> p k w", k=2))
            last.then_inc(w_set, 1)

            def floats(L, p, macro):
                prep = L.preps_before(p) + macro
                dve.wait_ge(L.turned, L.rounds * prep + 1)
                after(dve, dve_turn, L.meta_in, L.loaded(p, macro))
                v.tensor_copy(ends_f[0:ROWS], raw_ends[0:ROWS])
                v.tensor_scalar(chosen[0:ROWS, :], row_of_all[:, ds(MACRO_ITEMS * macro, MACRO_ITEMS)], small[0:ROWS, 4:5],
                                None, ALU.is_equal)
                v.tensor_scalar(moved[:, :], ident[:, :], shift[:, ds(macro, 1)], None, ALU.mult).then_inc(L.floats, 1)

            def block_at(item):
                return dve.value_load(row_i[0:1, ds(item, 1)], min_val=0, max_val=NB - 1)

            def add_sums(L, p, item, a, at):
                width = P * (L.n + 1)
                if L.n == 0:
                    dve.wait_ge(L.sums, L.sums_before(p) + item + 1)
                dve.wait_ge(L.added, p * (NIT + LAG) + item + 1)
                v.tensor_tensor(agg[:, ds(at * width, width)], bank[4 + a][:, 0:width],
                                agg[:, ds(at * width, width)], ALU.add).then_inc(L.added, 1)

            def walk_chunk(L, p, m, c):
                chunk = m * CHUNKS + c
                for j in range(ITEMS):
                    a = j % 2
                    item = chunk * ITEMS + j
                    col = ITEMS * (chunk % (2 * CHUNKS)) + j
                    at = block_at(item)
                    if L.n == 0:
                        add_sums(L, p, item, a, at)
                        for k in range(2):
                            last = v.tensor_scalar(hot[:, a, k, :], iota_free[:, :], dst_t[:, k, ds(col, 1)],
                                                   w_edge[:, k, ds(col, 1)], ALU.is_equal, ALU.mult)
                        last.then_inc(L.hot_ready, 1)
                        continue
                    if j % 2 == 0:
                        dve.wait_ge(L.quad[j // 2], 64 * (p * NCH + chunk) + 64)
                    to = scaled[:, j % PLACES]
                    part_i = to.rearrange("p (c k m) u -> p k c m u", c=2, k=2)
                    v.tensor_tensor(part_i[:, :, :, 7, :],
                                    rows[:, 2 * j:2 * j + 2, :].rearrange("p k (c u) -> p k c u", u=MUL)[:, :, 0:4:3, :],
                                    b_y2[:, :, ds(ITEMS * c + j, 1)].unsqueeze(3).to_broadcast([P, 2, 2, MUL]),
                                    ALU.mult).then_inc(L.third, 1)
                    dve.wait_ge(L.sums, L.sums_before(p) + item + 1)
                    v.tensor_tensor(hot[:, a, :, :], b_iota.unsqueeze(1).to_broadcast([P, 2, P]),
                                    dst_t[:, :, ds(col, 1)].to_broadcast([P, 2, P]), ALU.is_equal)
                    dve.wait_ge(L.third, p * NIT + item + 1)
                    dve.wait_ge(L.scaled, p * NIT + item + 1)
                    v.tensor_reduce(to[:, 4:16:8, :], part_i[:, :, 1, 5:8, :].rearrange("p k i u -> p k u i"),
                                    axis=AX.X, op=ALU.add).then_inc(L.dots, 1)
                    add_sums(L, p, item, a, at)
                    dve.wait_ge(L.weights, p * (NIT + 1) + item + 1)
                    four = to[:, 0:16, :].rearrange("p (r c) u -> p r c u", r=4)
                    wts = b_w[a][:, 0:2 * P].rearrange("p (g r u) -> p g r u", g=2, r=4)
                    v.tensor_tensor(msg[:, a, :, 1:4, :], four[:, :, 1:4, :],
                                    wts[:, 0].unsqueeze(2).to_broadcast([P, 4, 3, MUL]), ALU.mult)
                    dve.wait_ge(L.dots, p * NIT + item + 1)
                    v.tensor_tensor(msg[:, a, :, 0, :], four[:, :, 0, :], wts[:, 1], ALU.mult
                                    ).then_inc(L.mixed, 1)

            for L in layers:
                if L.n == 0:
                    dve.wait_ge(agg_zeroed, 1)
                    dve.sem_inc(L.added, 1)
                else:
                    link(v.memset(flag[:, 3:4], 0.0))
                    make_plan(L, 0)
                    v.tensor_copy(b_iota, iota_free[:, :])
                    dve.wait_ge(table_ready, 2)
                    link(v.memset(agg[:, NB * P:NB * P + 4 * GW], 0.0))
                    dve.wait_ge(agg_zeroed, NBG + 2)
                    dve.sem_inc(L.added, 1)
                with dve.Fori(0, passes) as p:
                    floats(L, p, 0)
                    with dve.Fori(0, MACROS) as m:
                        floats(L, p, m + 1)
                        after(dve, dve_turn, L.turned_out, L.rounds * (L.preps_before(p) + m + 1) + 1)
                        if L.n == 1:
                            v.tensor_copy(b_y2, y_edge[:, 3, :, ds((m % 2) * MACRO_ITEMS, MACRO_ITEMS)]).then_inc(L.y_set, 1)
                            after(dve, dve_turn, L.y_set, p * MACROS + m + 1)
                        with dve.Fori(0, CHUNKS) as c:
                            walk_chunk(L, p, m, c)
                    for a in range(LAG):
                        at = block_at(NIT + a)
                        if L.n == 1:
                            dve.wait_ge(L.sums, L.sums_before(p) + NIT + a + 1)
                        add_sums(L, p, NIT + a, a, at)
                    make_plan(L, p + 1)
                dve.wait_ge(L.plan_step, 2 * passes + 2)
                if L.n == 0:
                    dve.wait_ge(biased, NBG)
                dve.wait_ge(L.added, 1 + (NIT + LAG) * passes)
                dve.sem_inc(L.walked, 1)

                if L.n == 0:
                    dve.sem_inc(x1_ready, 1)
                    dve.sem_inc(h_copied, 1)

                    def add_x(t):
                        dve.wait_ge(lin_ready, NH * t + 2 * NH)
                        for h, (a, z) in enumerate(HALVES):
                            last = v.tensor_tensor(arena[:, ds(t * GW + a, z - a)], bank[h][:, 0:z - a],
                                                   arena[:, ds(t * GW + a, z - a)], ALU.add)
                        last.then_inc(x1_ready, 1)
                        after(dve, dve_turn, x1_ready, t + 2)

                    def copy_turned_rows(t):
                        dve.wait_ge(up_ready, t + 1)
                        dve.wait_ge(h_turned, t + 2)
                        for h, (a, z) in enumerate(HALVES):
                            last = v.tensor_copy(h_turn[:, a:z], bank[2 + h][:, 0:z - a])
                        last.then_inc(h_copied, 1)

                    add_x(0)
                    row_stats(0, NBG)
                    row_scales(NBG)
                    with dve.Fori(0, NBG - 1) as t:
                        add_x(t + 1)
                        row_stats(t + 1, NBG + t + 1)
                        copy_turned_rows(t)
                        row_scales(NBG + t + 1)
                    copy_turned_rows(NBG - 1)

            dve.sem_inc(fin_out, NH)
            dve.sem_inc(fin_saved, 2)
            with dve.Fori(0, NBG) as t:
                dve.wait_ge(fin_saved, t + 1)
                dve.wait_ge(fin_x, 16 * t + 16)
                for h, (a, z) in enumerate(HALVES):
                    dve.wait_ge(fin_ready, NH * t + NH + h + 1)
                    v.scalar_tensor_tensor(out=fin[:, ds(2 * GW + (t % 2) * GW + a, z - a)], in0=bank[h][:, 0:z - a],
                                           scalar=INV_OUT, in1=fin[:, ds((t % 2) * GW + a, z - a)], op0=ALU.mult,
                                           op1=ALU.add).then_inc(fin_out, 1)

        @block.tensor
        def _(pe):
            mm = nc.tensor.matmul
            pe.wait_ge(votes, 1)
            mm(bank[0][:, 0:2], ones[0:R1, :], small[0:R1, 0:2], start=True, stop=True).then_inc(counted, 1)
            total = hot[:, 1, (C2 - 1) % 2, 0:NB - 1]
            mm(bank[1][:, 0:NB - 1], ones[0:R2, :], total[0:R2, :], start=True, stop=True).then_inc(counted, 1)
            nc.tensor.transpose(bank[3][:, 0:P], w_t[:, :], ident[:, :]).then_inc(counted, 1)
            pe.wait_ge(votes, 2)
            mm(bank[2][:, 0:COLS], ones[0:1, :], first_pair[0:1, :], start=True, stop=True).then_inc(counted, 1)
            pe.wait_ge(votes, 3)
            nc.tensor.transpose(bank[2][:, 0:P], hot[:, 1, 0, :], ident[:, :]).then_inc(counted, 1)
            pe.wait_ge(passes_ready, 1)
            passes = pe.value_load(small_i[0:1, 2:3], min_val=1, max_val=NB)

            pe.wait_ge(w_set, 1)

            def turn(L, p, macro, r):
                prep = L.preps_before(p) + macro
                b_turn = b_turns[r % 2]
                after(pe, pe_turn, L.turned_out, L.rounds * prep + max(r, 1))
                after(pe, pe_turn, L.floats, prep + 1)
                if r >= 2:
                    for i in range(8):
                        e = 8 * (r - 2) + i
                        last = mm(b_turn[:, 64 * i:64 * i + 64], raw_ef[:, e, :, :].rearrange("p k w -> p (k w)"),
                                  chosen[0:ROWS, :], start=True, stop=True)
                else:
                    ends = ends_f.rearrange("p s (k e) -> p s k e", k=2)
                    y = raw_ea.rearrange("p (k e c) -> p c k e", k=2, c=4)
                    w = raw_w[:, :].rearrange("p (k e) -> p k e", k=2)
                    of = [[ends[:, 0], ends[:, 1], w if L.n == 0 else y[:, 0]], [y[:, 1], y[:, 2], y[:, 3]]][r]
                    for i, pairs in enumerate(of):
                        is_dst = (r, i) == (0, 1)
                        for k in range(2):
                            to = b_turn[:, P * i + MACRO_ITEMS * k:P * i + MACRO_ITEMS * (k + 1)]
                            if is_dst:
                                mm(to, ones[:, :], moved[:, MACRO_ITEMS * k:MACRO_ITEMS * (k + 1)], start=True, stop=False)
                            last = mm(to, pairs[0:ROWS, k, :], chosen[0:ROWS, :],
                                      start=not is_dst, stop=True)
                last.then_inc(L.turned, 1)

            def hidden1(L, p, macro, r, chunk, n_before):
                pe.wait_ge(L.turned_out, L.rounds * (L.preps_before(p) + macro + 1) + 1)
                pe.wait_ge(L.mlp_out, n_before + 1)
                col = ITEMS * (chunk % (2 * CHUNKS))
                for e in range(4):
                    last = mm(b_mlp[:, P * e:P * (e + 1)], a1_blocks[:, 4 * r + e, :], ef_t[:, :, ds(col, ITEMS)],
                              start=True, stop=True)
                last.then_inc(L.mlp, 1)

            def hidden2(L, r, n_before):
                pe.wait_ge(L.mlp_out, n_before + 1)
                mm(b_mlp[:, :], a2_pair[:, :], hid1[:, 4 * r:4 * r + 4, :].rearrange("p q e -> p (q e)"),
                   start=True, stop=True).then_inc(L.mlp, 1)

            def edge_weights(L, p, j, item):
                pe.wait_ge(L.mixed, p * NIT + FREE + item - 1)
                mm(b_w[j % 2][:, 0:2 * P], hid2[:, j, :], a3_pair[:, :], start=True, stop=True).then_inc(L.weights, 1)

            for L in layers:
                if L.n == 1:
                    pe.wait_ge(up_out, NBG + 1)
                with pe.Fori(0, passes) as p:
                    pe.wait_ge(L.plan, p + 1)
                    for a in range(LAG):
                        mm(bank[4 + a][:, 0:2 * P], zeros[:, :], a1_blocks[:, 0:2, :].rearrange("p e h -> p (e h)"),
                           start=True, stop=True).then_inc(L.sums, 1)
                    for r in range(L.rounds):
                        turn(L, p, 0, r)
                    if L.n == 1:
                        done = p * (3 + 4 * NCH)
                        hidden1(L, p, 0, 0, 0, done)
                        hidden1(L, p, 0, 1, 0, done + 1)
                        hidden2(L, 0, done + 2)
                        pe.wait_ge(L.mlp_out, done + 4)
                        edge_weights(L, p, 0, 0)

                    def walk_chunk(m, c):
                        chunk = m * CHUNKS + c
                        done = p * (3 + 4 * NCH) + 3 + 4 * chunk
                        first = isinstance(c, int)
                        if L.n == 1:
                            hidden2(L, 1, done)
                        for j in range(ITEMS):
                            a = j % 2
                            item = chunk * ITEMS + j
                            if L.n == 1:
                                if j == 3:
                                    pe.wait_ge(L.mlp_out, done + 2)
                                if j == ITEMS - 1:
                                    pe.wait_ge(L.mlp_out, done + 5)
                                edge_weights(L, p, (j + 1) % ITEMS, item + 1)
                            if first and j in TURN_AT[:L.rounds]:
                                turn(L, p, m + 1, TURN_AT.index(j))
                            if L.n == 0 and j % 2 == 0:
                                pe.wait_ge(L.quad[j // 2], 64 * (p * NCH + chunk) + 64)
                            if L.n == 0:
                                pe.wait_ge(L.hot_ready, p * NIT + item + 1)
                            else:
                                pe.wait_ge(L.mixed, p * NIT + FREE + item + 1)
                            for half in range(L.n + 1):
                                for k in range(2):
                                    of = rows[:, 2 * j + k, :] if L.n == 0 else \
                                        msg[:, a, 2 * k + half, :, :].rearrange("p c u -> p (c u)")
                                    last = mm(bank[4 + a][:, P * half:P * (half + 1)], of, hot[:, a, k, :],
                                              start=k == 0, stop=k == 1)
                            last.then_inc(L.sums, 1)
                            if L.n == 1 and j in (0, 2):
                                hidden1(L, p, m if first else m + 1, j // 2, chunk + 1, done + 1 + j // 2)
                            if L.n == 1 and j == 4:
                                hidden2(L, 0, done + 3)

                    with pe.Fori(0, MACROS) as m:
                        walk_chunk(m, 0)
                        with pe.Fori(1, CHUNKS) as c:
                            walk_chunk(m, c)

                if L.n == 0:
                    pe.sem_inc(lin_ready, NH)
                    pe.sem_inc(h_turned, 1)
                    pe.sem_inc(up_ready, 1)

                    def linear(t):
                        pe.wait_ge(x1_ready, t + 1)
                        for h in range(NH):
                            pe.wait_ge(sums_in, NH * t + h + 1)
                            for g in blocks_in(h):
                                h, at = where(g)
                                last = mm(bank[h][:, at:at + P], sums_st[:, g * P:(g + 1) * P], w_t[:, :],
                                          start=True, stop=True)
                            last.then_inc(lin_ready, 1)

                    def turn_rows(t):
                        pe.wait_ge(h_copied, t + 1)
                        pe.wait_ge(normed, NBG + t + 2)
                        for g in range(GB):
                            h, at = where(g)
                            last = nc.tensor.transpose(bank[2 + h][:, at:at + P], h_st[:, g * P:(g + 1) * P], ident[:, :])
                        last.then_inc(h_turned, 1)

                    def table_rows(t):
                        pe.wait_ge(up_out, t + 1)
                        pe.wait_ge(h_copied, t + 2)
                        for g in range(GB):
                            h, at = where(g)
                            last = mm(bank[4 + h][:, at:at + P], h_turn[:, g * P:(g + 1) * P], w_up[:, :],
                                      start=True, stop=True)
                        last.then_inc(up_ready, 1)

                    linear(0)
                    linear(1)
                    with pe.Fori(0, NBG - 2) as t:
                        turn_rows(t)
                        linear(t + 2)
                        table_rows(t)
                    for t in (NBG - 2, NBG - 1):
                        turn_rows(t)
                        table_rows(t)

            pe.sem_inc(fin_ready, NH)
            with pe.Fori(0, NBG) as t:
                for h in range(NH):
                    pe.wait_ge(fin_out, NH * t + h + 1)
                    pe.wait_ge(fin_staged, NH * t + h + 1)
                    for g in blocks_in(h):
                        at = where(g)[1]
                        for k in range(2):
                            last = mm(bank[h][:, at:at + P], fin_sums[:, (2 * g + k) * P:(2 * g + k + 1) * P], w_out[:, k, :],
                                      start=k == 0, stop=k == 1)
                    last.then_inc(fin_ready, 1)


_INS = ['x', 'src', 'dst', 'edge_attr_4', 'edge_attr_8', 'edge_weight', 'L0_gnn_W', 'L0_gnn_b', 'L1_gnn_W_up_s',
        'L1_gnn_W_up_v', 'L1_gnn_A1', 'L1_gnn_b1', 'L1_gnn_A2', 'L1_gnn_b2', 'L1_gnn_A3', 'L1_gnn_W_out_s',
        'L1_gnn_W_out_v']


def kernel(**inputs):
    import numpy as _np
    import concourse.bacc as _bacc
    from concourse import mybir as _mybir
    from concourse.bass_utils import run_bass_kernel_spmd as _run

    nc = _bacc.Bacc("TRN2", target_bir_lowering=False, num_devices=1)
    arrays, args = {}, []
    for name in _INS:
        a = _np.ascontiguousarray(inputs[name])
        arrays[f"in_{name}_dram"] = a
        args.append(nc.dram_tensor(f"in_{name}_dram", a.shape, _mybir.dt.from_np(a.dtype), kind="ExternalInput").ap())
    shape = inputs['x'].shape
    args.append(nc.dram_tensor("out_0_dram", shape, _mybir.dt.float32, kind="ExternalOutput").ap())
    build_gnn(nc, *args)
    r = _run(nc, [arrays], core_ids=[0])
    return r.results[0]["out_0_dram"]
```
